# Optimizing a Trainium2 kernel written in Bass

```python
import numpy as np
import jax
import jax.numpy as jnp

def _softmax(x, axis=-1):
    return jax.nn.softmax(x, axis=axis)

def _gelu(x):
    return jax.nn.gelu(x, approximate=True)

def _silu(x):
    return jax.nn.silu(x)

def _sigmoid(x):
    return jax.nn.sigmoid(x)

def _layernorm(x, axis=-1, eps=1e-05):
    m = jnp.mean(x, axis=axis, keepdims=True)
    v = jnp.var(x, axis=axis, keepdims=True)
    return (x - m) / jnp.sqrt(v + eps)

def _scatter_add(tgt, idx, src, axis=0):
    return tgt.at[idx].add(src)

def _segment_sum(src, seg, n):
    return jax.ops.segment_sum(src, seg, n)
kernel_name = 'mk_vit_tower_d2_tok_img1024_r4_e45bf7'

def setup_inputs(seed: int=0):
    np.random.seed(seed)
    _w = jnp.asarray

    def _rec_inputs():
        import jax
        import jax.numpy as jnp
        _rk = jax.random.key(seed)
        x = -0.00016672 + 0.999947 * jax.random.normal(jax.random.fold_in(_rk, 1), (32, 3, 96, 96), jnp.float32)
        return x
    x = _rec_inputs()

    def _L0_tok_setup():
        import jax, jax.numpy as jnp
        import numpy as np
        B, C, H, W = (64, 3, 96, 96)
        P = 16
        HP, WP = (H // P, W // P)
        N = HP * WP
        F = C * P * P
        D = 256
        key = jax.random.key(seed)
        k1, k2, k3, k4, k5 = jax.random.split(key, 5)
        data = jax.random.normal(k1, (B, C, H, W), dtype=jnp.float32)
        lim = 1.0 / np.sqrt(F)
        W_lin = jax.random.uniform(k2, (D, F), minval=-lim, maxval=lim, dtype=jnp.float32)
        b_lin = jax.random.uniform(k3, (D,), minval=-lim, maxval=lim, dtype=jnp.float32)
        class_token = jax.random.normal(k4, (1, 1, D), dtype=jnp.float32)
        position_embeddings = jax.random.normal(k5, (1, N + 1, D), dtype=jnp.float32)
        return {'data': data, 'W_lin': W_lin, 'b_lin': b_lin, 'class_token': class_token, 'position_embeddings': position_embeddings}
    _L0_tok_all = _L0_tok_setup()
    _L0_tok_in = {k: v for k, v in _L0_tok_all.items() if k in ('W_lin', 'b_lin', 'class_token', 'position_embeddings')}
    del _L0_tok_all

    def _L0_attn_setup():
        import jax, jax.numpy as jnp
        import numpy as np
        D_MODEL = 256
        N_HEADS = 16
        D_HEAD = 64
        BATCH = 4
        SEQ = 512
        NEG = -1000000000.0
        key = jax.random.key(seed)
        k1, k2, k3, k4, k5 = jax.random.split(key, 5)
        x = jax.random.normal(k1, (BATCH, SEQ, D_MODEL), dtype=jnp.float32)
        std = 0.02
        wq = jax.random.normal(k2, (N_HEADS, D_HEAD, D_MODEL), dtype=jnp.float32) * std
        wk = jax.random.normal(k3, (N_HEADS, D_HEAD, D_MODEL), dtype=jnp.float32) * std
        wv = jax.random.normal(k4, (N_HEADS, D_HEAD, D_MODEL), dtype=jnp.float32) * std
        wo = jax.random.normal(k5, (D_MODEL, N_HEADS * D_HEAD), dtype=jnp.float32) * std
        return {'x': x, 'wq': wq, 'wk': wk, 'wv': wv, 'wo': wo}
    _L0_attn_all = _L0_attn_setup()
    _L0_attn_in = {k: v for k, v in _L0_attn_all.items() if k in ('wq', 'wk', 'wv', 'wo')}
    del _L0_attn_all

    def _L0_ffn_setup():
        import jax, jax.numpy as jnp
        import numpy as np
        MANT_BITS = 8
        _PWL_X = jnp.linspace(-4.0, 4.0, 33, dtype=jnp.float32)
        _PWL_Y = 0.5 * _PWL_X * (1.0 + jax.lax.erf(_PWL_X / jnp.sqrt(jnp.float32(2.0))))

        def float2fix(x, mantissa_bits):
            s = jnp.float32(2.0 ** mantissa_bits)
            q = jnp.round(x * s) / s
            return x + jax.lax.stop_gradient(q - x)

        def pwlin_gelu_basic(x, mantissa_bits_in, mantissa_bits_out):
            xq = float2fix(x, mantissa_bits_in)
            y = jnp.interp(xq, _PWL_X, _PWL_Y)
            y = jnp.where(xq > 4.0, xq, jnp.where(xq < -4.0, jnp.float32(0.0), y))
            return float2fix(y, mantissa_bits_out)
        key = jax.random.key(seed)
        k_x, k_w1, k_b1, k_w2, k_b2 = jax.random.split(key, 5)
        dim, ff_dim = (256, 1024)
        B, S = (32, 128)
        sc1 = 1.0 / np.sqrt(dim)
        sc2 = 1.0 / np.sqrt(ff_dim)
        return {'x': jax.random.normal(k_x, (B, S, dim), dtype=jnp.float32), 'w1': jax.random.uniform(k_w1, (dim, ff_dim), jnp.float32, -sc1, sc1), 'b1': jax.random.uniform(k_b1, (ff_dim,), jnp.float32, -sc1, sc1), 'w2': jax.random.uniform(k_w2, (ff_dim, dim), jnp.float32, -sc2, sc2), 'b2': jax.random.uniform(k_b2, (dim,), jnp.float32, -sc2, sc2)}
    _L0_ffn_all = _L0_ffn_setup()
    _L0_ffn_in = {k: v for k, v in _L0_ffn_all.items() if k in ('w1', 'b1', 'w2', 'b2')}
    del _L0_ffn_all

    def _L1_attn_setup():
        import jax, jax.numpy as jnp
        import numpy as np
        B, S, D = (2, 512, 256)
        H, DH = (16, 64)
        SCALE = DH ** (-0.5)
        key = jax.random.key(seed)
        ks = jax.random.split(key, 5)

        def w(k, shape):
            return jax.random.normal(k, shape, dtype=jnp.float32) * 0.02
        return {'x': jax.random.normal(ks[0], (B, S, D), dtype=jnp.float32), 'Wq': w(ks[1], (D, H * DH)), 'Wk': w(ks[2], (D, H * DH)), 'Wv': w(ks[3], (D, H * DH)), 'Wo': w(ks[4], (H * DH, D)), 'bo': jnp.zeros((D,), dtype=jnp.float32)}
    _L1_attn_all = _L1_attn_setup()
    _L1_attn_in = {k: v for k, v in _L1_attn_all.items() if k in ('Wq', 'Wk', 'Wv', 'Wo', 'bo')}
    del _L1_attn_all

    def _L1_ffn_setup():
        import jax, jax.numpy as jnp
        import numpy as np
        B, L, D = (4, 256, 256)
        E, H = (8, 1024)
        CAPACITY = 6
        key = jax.random.key(seed)
        ks = jax.random.split(key, 6)
        x = jax.random.normal(ks[0], (B, L, D), dtype=jnp.float32)
        gate_weight = jax.random.normal(ks[1], (E, D), dtype=jnp.float32) * 0.006
        w1 = jax.random.normal(ks[2], (E, H, D), dtype=jnp.float32) * 0.02
        b1 = jnp.zeros((E, H), dtype=jnp.float32)
        w2 = jax.random.normal(ks[3], (E, D, H), dtype=jnp.float32) * 0.02
        b2 = jnp.zeros((E, D), dtype=jnp.float32)
        return {'x': x, 'gate_weight': gate_weight, 'w1': w1, 'b1': b1, 'w2': w2, 'b2': b2}
    _L1_ffn_all = _L1_ffn_setup()
    _L1_ffn_in = {k: v for k, v in _L1_ffn_all.items() if k in ('gate_weight', 'w1', 'b1', 'w2', 'b2')}
    del _L1_ffn_all
    return {'x': x, 'L0_tok_W_lin': _L0_tok_in['W_lin'], 'L0_tok_b_lin': _L0_tok_in['b_lin'], 'L0_tok_class_token': _L0_tok_in['class_token'], 'L0_tok_position_embeddings': _L0_tok_in['position_embeddings'], 'L0_attn_wq': _L0_attn_in['wq'], 'L0_attn_wk': _L0_attn_in['wk'], 'L0_attn_wv': _L0_attn_in['wv'], 'L0_attn_wo': _L0_attn_in['wo'], 'L0_ffn_w1': _L0_ffn_in['w1'], 'L0_ffn_b1': _L0_ffn_in['b1'], 'L0_ffn_w2': _L0_ffn_in['w2'], 'L0_ffn_b2': _L0_ffn_in['b2'], 'L1_attn_Wq': _L1_attn_in['Wq'], 'L1_attn_Wk': _L1_attn_in['Wk'], 'L1_attn_Wv': _L1_attn_in['Wv'], 'L1_attn_Wo': _L1_attn_in['Wo'], 'L1_attn_bo': _L1_attn_in['bo'], 'L1_ffn_gate_weight': _L1_ffn_in['gate_weight'], 'L1_ffn_w1': _L1_ffn_in['w1'], 'L1_ffn_b1': _L1_ffn_in['b1'], 'L1_ffn_w2': _L1_ffn_in['w2'], 'L1_ffn_b2': _L1_ffn_in['b2']}

def reference(x, L0_tok_W_lin, L0_tok_b_lin, L0_tok_class_token, L0_tok_position_embeddings, L0_attn_wq, L0_attn_wk, L0_attn_wv, L0_attn_wo, L0_ffn_w1, L0_ffn_b1, L0_ffn_w2, L0_ffn_b2, L1_attn_Wq, L1_attn_Wk, L1_attn_Wv, L1_attn_Wo, L1_attn_bo, L1_ffn_gate_weight, L1_ffn_w1, L1_ffn_b1, L1_ffn_w2, L1_ffn_b2):
    import jax
    import jax.numpy as jnp

    def _L0_tok_ref(data, W_lin, b_lin, class_token, position_embeddings):
        import jax, jax.numpy as jnp
        import numpy as np
        B, C, H, W = (64, 3, 96, 96)
        P = 16
        HP, WP = (H // P, W // P)
        N = HP * WP
        F = C * P * P
        D = 256
        b = data.shape[0]
        x = data.reshape(b, C, HP, P, WP, P)
        x = x.transpose(0, 2, 4, 1, 3, 5).reshape(b, N, F)
        x = jnp.einsum('bnf,df->bnd', x, W_lin) + b_lin
        cls = jnp.broadcast_to(class_token, (b, 1, D))
        out = jnp.concatenate([cls, x], axis=1) + position_embeddings
        return out

    def _L0_attn_ref(x, wq, wk, wv, wo):
        import jax, jax.numpy as jnp
        import numpy as np
        D_MODEL = 256
        N_HEADS = 16
        D_HEAD = 64
        BATCH = 4
        SEQ = 512
        NEG = -1000000000.0
        b, s, _ = x.shape
        scale = jnp.sqrt(jnp.asarray(D_HEAD, x.dtype))
        q = jnp.einsum('bsd,hed->bhse', x, wq)
        k = jnp.einsum('bsd,hed->bhse', x, wk)
        v = jnp.einsum('bsd,hed->bhse', x, wv)
        scores = jnp.einsum('bhse,bhte->bhst', q, k) / scale
        causal_mask = jnp.triu(jnp.ones((s, s), dtype=bool), k=1)
        scores = jnp.where(causal_mask, jnp.asarray(NEG, scores.dtype), scores)
        weights = jax.nn.softmax(scores, axis=-1)
        heads = jnp.einsum('bhst,bhte->bhse', weights, v)
        concat = heads.transpose(0, 2, 1, 3).reshape(b, s, N_HEADS * D_HEAD)
        return concat @ wo.T

    def _L0_ffn_ref(x, w1, b1, w2, b2):
        import jax, jax.numpy as jnp
        import numpy as np
        MANT_BITS = 8
        _PWL_X = jnp.linspace(-4.0, 4.0, 33, dtype=jnp.float32)
        _PWL_Y = 0.5 * _PWL_X * (1.0 + jax.lax.erf(_PWL_X / jnp.sqrt(jnp.float32(2.0))))

        def float2fix(x, mantissa_bits):
            s = jnp.float32(2.0 ** mantissa_bits)
            q = jnp.round(x * s) / s
            return x + jax.lax.stop_gradient(q - x)

        def pwlin_gelu_basic(x, mantissa_bits_in, mantissa_bits_out):
            xq = float2fix(x, mantissa_bits_in)
            y = jnp.interp(xq, _PWL_X, _PWL_Y)
            y = jnp.where(xq > 4.0, xq, jnp.where(xq < -4.0, jnp.float32(0.0), y))
            return float2fix(y, mantissa_bits_out)
        h = jnp.einsum('bsd,df->bsf', x, w1) + b1
        h = float2fix(h, MANT_BITS)
        h = pwlin_gelu_basic(h, MANT_BITS, MANT_BITS)
        h = float2fix(h, MANT_BITS)
        out = jnp.einsum('bsf,fd->bsd', h, w2) + b2
        return float2fix(out, MANT_BITS)

    def _L1_attn_ref(x, Wq, Wk, Wv, Wo, bo):
        import jax, jax.numpy as jnp
        import numpy as np
        B, S, D = (2, 512, 256)
        H, DH = (16, 64)
        SCALE = DH ** (-0.5)
        b, s, _ = x.shape
        q = (x @ Wq).reshape(b, s, H, DH)
        k = (x @ Wk).reshape(b, s, H, DH)
        v = (x @ Wv).reshape(b, s, H, DH)
        scores = jnp.einsum('bqhd,bkhd->bhqk', q, k) * SCALE
        attn = jax.nn.softmax(scores, axis=-1)
        out = jnp.einsum('bhqk,bkhd->bqhd', attn, v).reshape(b, s, H * DH)
        return out @ Wo + bo

    def _L1_ffn_ref(x, gate_weight, w1, b1, w2, b2):
        import jax, jax.numpy as jnp
        import numpy as np
        B, L, D = (4, 256, 256)
        E, H = (8, 1024)
        CAPACITY = 6
        logits = jnp.einsum('bld,ed->ble', x, gate_weight)
        expert_k = B * L * CAPACITY
        kth_val = jnp.sort(logits.reshape(-1))[expert_k - 1]
        mask = (logits >= kth_val).astype(x.dtype)
        gates = logits * mask
        h = jax.nn.gelu(jnp.einsum('bld,ehd->bleh', x, w1) + b1, approximate=True)
        y = jnp.einsum('bleh,edh->blde', h, w2) + b2.T[None, None]
        out = jnp.einsum('blde,ble->bld', y, gates)
        return out
    h = _L0_tok_ref(x, L0_tok_W_lin, L0_tok_b_lin, L0_tok_class_token, L0_tok_position_embeddings)
    h = h + _L0_attn_ref(_layernorm(h, axis=-1), L0_attn_wq, L0_attn_wk, L0_attn_wv, L0_attn_wo)
    h = h + _L0_ffn_ref(_layernorm(h, axis=-1), L0_ffn_w1, L0_ffn_b1, L0_ffn_w2, L0_ffn_b2)
    h = h + _L1_attn_ref(_layernorm(h, axis=-1), L1_attn_Wq, L1_attn_Wk, L1_attn_Wv, L1_attn_Wo, L1_attn_bo)
    h = h + _L1_ffn_ref(_layernorm(h, axis=-1), L1_ffn_gate_weight, L1_ffn_w1, L1_ffn_b1, L1_ffn_w2, L1_ffn_b2)
    return h

_drawn_inputs = setup_inputs


def setup_inputs(seed=0):
    import zlib

    import numpy as np

    out = dict(_drawn_inputs(seed))
    spreads = {'L1_attn_bo': (0.0, 0.1), 'L1_ffn_b1': (0.0, 0.8), 'L1_ffn_b2': (0.0, 0.552)}
    factors = {'L0_tok_b_lin': 2.977,
     'L0_attn_wq': 8.0,
     'L0_attn_wk': 8.0,
     'L0_ffn_b1': 5.296,
     'L0_ffn_b2': 3.683,
     'L1_attn_Wq': 8.0,
     'L1_attn_Wk': 8.0,
     'L1_ffn_gate_weight': 3.015,
     'L1_ffn_w1': 3.628,
     'L1_ffn_w2': 3.337}
    for name, (base, spread) in spreads.items():
        noise = np.random.default_rng([zlib.crc32(name.encode()), seed]).standard_normal(out[name].shape)
        drawn = base * np.exp(spread * noise) if base else spread * noise
        out[name] = jnp.asarray(drawn.astype(out[name].dtype))
    for name, factor in factors.items():
        out[name] = (out[name] * factor).astype(out[name].dtype)
    return out
```

```python
from contextlib import ExitStack

import concourse.bass as bass
from concourse import mybir

F32 = mybir.dt.float32
F32R = mybir.dt.float32r
BF16 = mybir.dt.bfloat16
I32 = mybir.dt.int32
ALU = mybir.AluOpType
ACT = mybir.ActivationFunctionType
AX_X = mybir.AxisListType.X

P = 128
B, C, IMG, PATCH = 32, 3, 96, 16
SIDE = IMG // PATCH
TOK = SIDE * SIDE + 1
D = 256
KD = D // P
KF = C * PATCH * PATCH // P
HEADS, DH = 16, 64
HD = HEADS * DH
KO = HD // P
FF = 1024
KH = FF // P
E = 8
TOPK = 4 * 256 * 6
NLOG = B * TOK * E

GI = 3
GW = GI * TOK + 1
NG = -(-B // GI)
NTOK = [min(GI, B - g * GI) * TOK for g in range(NG)]
T = (NG - 1) * GW + NTOK[-1]
GC = 3
CW = GC * GW
NC = -(-NG // GC)
CHUNKS = [(c * CW, min(CW, T - c * CW)) for c in range(NC)]
GROUPS = [list(range(c * GC, min((c + 1) * GC, NG))) for c in range(NC)]
QH = 4
NQ = HEADS // QH
QUADS = [(c, g, t) for c in range(NC) for g in GROUPS[c] for t in range(NQ)]

EPS = 1e-5
UNIT = 256.0
MAGIC = 1.5 * 2.0 ** 23
KNOT = 64.0
MAGIC_KNOT = MAGIC * KNOT
BIG = 3.4028234663852886e38

S_POS = 0
S_CLS = S_POS + KD * TOK
S_BLIN = S_CLS + KD
S_BO = S_BLIN + KD
S_B1F = S_BO + KD
S_B2F = S_B1F + KH
S_B1M = S_B2F + KD
S_B2M = S_B1M + E * KH
S_GATE = S_B2M + KD * E
S_END = S_GATE + KD * E

PIECE = KD * 1024
WSLOTS = 4


def vit_tower(nc, x, w_lin, weights, small, ident_in, mask_in, out):
    with ExitStack() as ctx:
        def sb(name, shape, dt=F32):
            return ctx.enter_context(nc.sbuf_tensor(name, shape, dt))

        def sem(name):
            return ctx.enter_context(nc.semaphore(name))

        h = sb("h", [P, KD, T])
        xn = sb("xn", [P, 2, KD, T], F32R)
        wslot = sb("wslot", [P, WSLOTS, 2, PIECE], F32R)
        raw = sb("raw", [P, 2, PIECE])
        hid = sb("hid", [P, 2, 2, KH * CW], F32R)
        work = sb("work", [P, HEADS, CW])
        vbuf = sb("vbuf", [P, 2, HD])
        probs = sb("probs", [P, 3, QH * GW])
        probsT = sb("probsT", [P, 2, QH * GW])
        xc = sb("xc", [P, 2, KD, CW])
        sq = sb("sq", [P, KD, CW])
        rs = sb("rs", [P, CW])
        rt = sb("rt", [P, CW])
        prm = sb("prm", [P, S_END])
        addT = sb("addT", [P, KD, TOK])
        b1u = sb("b1u", [P, KH])
        b2u = sb("b2u", [P, KD])
        gateR = sb("gateR", [P, 2, KD * E], F32R)
        ident = sb("ident", [P, P])
        identb = sb("identb", [P, P], BF16)
        maskf = sb("maskf", [P, 2, GW])
        maskb = sb("maskb", [P, 2, QH, GW], BF16)
        mean_w = sb("mean_w", [P, P])
        c_eps = sb("c_eps", [P, 1])
        c_zero = sb("c_zero", [P, 1])
        c_knot = sb("c_knot", [P, 1])
        negmax = sb("negmax", [P, 4 * QH])
        maxes = sb("maxes", [P, 4 * QH])
        sums = sb("sums", [P, 4 * QH])
        rsum = sb("rsum", [P, 4 * QH])
        logits = sb("logits", [P, NG * E])
        keys = sb("keys", [P, NG * E])
        below = sb("below", [P, NG * E])
        gates = sb("gates", [P, NG * E])
        count = sb("count", [P, 2])
        sign = sb("sign", [P, 1])
        rank = sb("rank", [P, 1])
        kth = sb("kth", [P, 1])
        found = sb("found", [P, 1], I32)
        tryb = sb("tryb", [P, 1], I32)
        newb = sb("newb", [P, 1], I32)

        bank = {n: ctx.enter_context(nc.psum_tensor(n, [P, 512], F32))
                for n in ("D0", "D1", "S0", "S1", "T0", "T1", "O0", "O1")}
        BD = [bank["D0"], bank["D1"]]
        BS = [bank["S0"], bank["S1"]]
        BT = [bank["T0"], bank["T1"]]
        BO = [bank["O0"], bank["O1"]]
        BH = BD + BS

        small_in = sem("small_in")
        mats_in = sem("mats_in")
        raw_in = [sem("raw_in0"), sem("raw_in1")]
        high_ready = sem("high_ready")
        start_split = sem("start_split")
        pool_high = sem("pool_high")
        pool_split = sem("pool_split")
        dve_line = sem("dve_line")
        act_line = sem("act_line")
        pool_line = sem("pool_line")
        consts = sem("consts")
        params = sem("params")
        masks = sem("masks")
        emb_mm = sem("emb_mm")
        h_set = sem("h_set")
        pads = sem("pads")
        ln_mean = [sem(f"ln_mean{n}") for n in range(4)]
        ln_xc = [sem(f"ln_xc{n}") for n in range(4)]
        ln_sq = [sem(f"ln_sq{n}") for n in range(4)]
        ln_var = [sem(f"ln_var{n}") for n in range(4)]
        ln_ln = [sem(f"ln_ln{n}") for n in range(4)]
        ln_rs = [sem(f"ln_rs{n}") for n in range(4)]
        ln_out = [sem(f"ln_out{n}") for n in range(4)]
        qk_mm = [sem(f"qk_mm{n}") for n in range(2)]
        qk_act = [sem(f"qk_act{n}") for n in range(2)]
        qk_dve = [sem(f"qk_dve{n}") for n in range(2)]
        v_mm = [sem(f"v_mm{n}") for n in range(2)]
        v_act = [sem(f"v_act{n}") for n in range(2)]
        v_dve = [sem(f"v_dve{n}") for n in range(2)]
        s_mm = [sem(f"s_mm{n}") for n in range(2)]
        s_max = [sem(f"s_max{n}") for n in range(2)]
        s_exp = [sem(f"s_exp{n}") for n in range(2)]
        p_norm = [sem(f"p_norm{n}") for n in range(2)]
        t_mm = [sem(f"t_mm{n}") for n in range(2)]
        t_dve = [sem(f"t_dve{n}") for n in range(2)]
        o_mm = [sem(f"o_mm{n}") for n in range(2)]
        o_high = [sem(f"o_high{n}") for n in range(2)]
        o_low = [sem(f"o_low{n}") for n in range(2)]
        out_mm = [sem(f"out_mm{n}") for n in range(2)]
        h_attn = [sem(f"h_attn{n}") for n in range(2)]
        ff1_mm = sem("ff1_mm")
        ff_t = sem("ff_t")
        ff_v = sem("ff_v")
        ff_abs = sem("ff_abs")
        ff_relu = sem("ff_relu")
        ff_knot = sem("ff_knot")
        ff_y0 = sem("ff_y0")
        ff_y1 = sem("ff_y1")
        ff_dy = sem("ff_dy")
        ff_frac = sem("ff_frac")
        ff_lin = sem("ff_lin")
        ff_q = sem("ff_q")
        ff_sum = sem("ff_sum")
        ff_hid = sem("ff_hid")
        ff2_mm = sem("ff2_mm")
        ff2_ev = sem("ff2_ev")
        h_ff = sem("h_ff")
        log_mm = sem("log_mm")
        cnt_ready = sem("cnt_ready")
        cnt_mm = sem("cnt_mm")
        gates_ready = sem("gates_ready")
        gb_mm = sem("gb_mm")
        gb_act = sem("gb_act")
        m1_mm = sem("m1_mm")
        m_gelu = sem("m_gelu")
        m_high = sem("m_high")
        m_hid = sem("m_hid")
        m2_mm = sem("m2_mm")
        m_y = sem("m_y")
        h_moe = sem("h_moe")
        stored = sem("stored")

        FIRST_W = 1 + NC
        NSTART = FIRST_W + 2
        NPIECE = FIRST_W + len(weights)

        def piece_split(i):
            return (start_split, i + 1) if i < NSTART else (pool_split, i - NSTART + 1)

        def piece_place(i):
            if i == 0:
                return [wslot[:, WSLOTS - 1, k, 0:KF * D] for k in range(2)]
            if i < FIRST_W:
                c = i - 1
                return [hid[:, c % 2, k, 0:KF * CHUNKS[c][1]] for k in range(2)]
            return [wslot[:, (i - FIRST_W) % WSLOTS, k, :] for k in range(2)]

        def piece_size(i):
            return KF * D if i == 0 else KF * CHUNKS[i - 1][1] if i < FIRST_W else PIECE

        def place_free(i):
            if i < FIRST_W:
                return (emb_mm, KD * (i - 2)) if i >= 3 else None
            j = i - FIRST_W
            if j < WSLOTS - 1:
                return None
            return [(emb_mm, KD * NC),
                    (qk_mm[0], 16 * (NC - 1) + 8), (qk_mm[0], 16 * NC), (v_mm[0], 2 * NG), (out_mm[0], KD * NC),
                    (ff1_mm, KH * NC), (ff2_mm, KD * NC),
                    (qk_mm[1], 16 * (NC - 1) + 8), (qk_mm[1], 16 * NC), (v_mm[1], 2 * NG), (out_mm[1], KD * NC),
                    ][j - 3] if j < 14 else ((m1_mm, m2_mm)[j % 2], (KH, KD)[j % 2] * NC * ((j - 14) // 2 + 1))

        W_QKVO = [0, 6]
        W_FF, W_MOE = 4, 10

        def weight(j, k, width):
            return wslot[:, j % WSLOTS, k, :].rearrange("p (a n) -> p a n", n=width)

        def wait_weight(eng, j):
            eng.wait_ge(*piece_split(FIRST_W + j))

        def heads(t):
            return [2 * QH * (t // 2) + t % 2 + 2 * i for i in range(QH)]

        def cols(g):
            return slice(g * GW, g * GW + NTOK[g])

        def ff_bufs(s):
            w = CHUNKS[s // KH][1]
            return [work[:, 5 * (s % 3) + k, 0:w] for k in range(5)]

        def ff_pool_diff(pool, s):
            v, a, kn, y0, y1 = ff_bufs(s)
            pool.wait_ge(ff_y1, s + 1)
            nc.gpsimd.tensor_tensor(y1, y1, y0, ALU.subtract).then_inc(ff_dy, 1)

        def ff_pool_sum(pool, s):
            v, a, kn, y0, y1 = ff_bufs(s)
            pool.wait_ge(ff_q, s + 1)
            nc.gpsimd.tensor_tensor(y0, y0, v, ALU.add).then_inc(ff_sum, 1)

        def moe_add(pool, e, c, dc):
            a, w = CHUNKS[c]
            j = (e * NC + c) * KD + dc
            pool.wait_ge(m_y, j + 1)
            if j >= KD * NC:
                pool.wait_ge(h_moe, j - KD * NC + 1)
            nc.gpsimd.tensor_tensor(h[:, dc, a:a + w], h[:, dc, a:a + w], moe_y(j)[:, 0:w],
                                    ALU.add).then_inc(h_moe, 1)

        def moe_g(s):
            return work[:, s % 4, :]

        def moe_y(j):
            return work[:, 4 + j % 4, :]

        def moe_gate(e, c):
            return work[:, 8 + (e % 2) * NC + c, :]

        def heads_out(k, c, t, a, nt):
            m = QH * (t // 2)
            return hid[:, c % 2, k, :].rearrange("p (m n) -> p m n", n=CW)[:, m:m + QH, a:a + nt]

        def out_pair(pair, nt):
            return BO[pair % 2][:, 0:QH * GW].rearrange("p (m n) -> p m n", n=GW)[:, :, 0:nt]

        block = ctx.enter_context(nc.Block())

        @block.sync
        def _(sp):
            sp.dma_start(prm[:, :], small).then_inc(small_in, 16)
            for i in range(NPIECE):
                if i >= 2:
                    sp.wait_ge(*piece_split(i - 2))
                n = piece_size(i)
                if i == 0:
                    src = w_lin
                elif i < FIRST_W:
                    a, w = CHUNKS[i - 1]
                    src = x[:, :, a:a + w]
                else:
                    src = weights[i - FIRST_W]
                dst = raw[:, i % 2, 0:n]
                if 0 < i < FIRST_W:
                    dst = dst.rearrange("p (k n) -> p k n", k=KF)
                sp.dma_start(dst, src).then_inc(raw_in[i % 2], 16)
                if i == 1:
                    sp.dma_start(ident[:, :], ident_in).then_inc(mats_in, 16)
                    sp.dma_start(maskf[:, :, :], mask_in).then_inc(mats_in, 16)
            for c, (a, w) in enumerate(CHUNKS):
                sp.wait_ge(h_moe, KD * NC * (E - 1) + KD * (c + 1))
                sp.dma_start(out[:, :, a:a + w], h[:, :, a:a + w]).then_inc(stored, 16)
            sp.wait_ge(stored, 16 * NC)

        @block.gpsimd
        def _(pool):
            nc.gpsimd.memset(mean_w[:, :], 1.0 / D).then_inc(consts, 1)
            nc.gpsimd.memset(c_eps[:, :], EPS).then_inc(consts, 1)
            nc.gpsimd.memset(c_zero[:, :], 0.0).then_inc(consts, 1)
            nc.gpsimd.memset(c_knot[:, :], -KNOT / UNIT).then_inc(consts, 1)
            nc.gpsimd.memset(logits[:, :], BIG).then_inc(consts, 1)
            nc.gpsimd.memset(keys[:, :], BIG).then_inc(consts, 1)
            nc.gpsimd.memset(gates[:, :], 0.0).then_inc(consts, 1)

            def split(i):
                pool.wait_ge(raw_in[i % 2], 16 * (i // 2 + 1))
                if place_free(i):
                    pool.wait_ge(*place_free(i))
                high, low = piece_place(i)
                nc.gpsimd.tensor_copy(high, raw[:, i % 2, :]).then_inc(pool_high, 1)
                pool.wait_ge(pool_high, i - NSTART + 1)
                nc.gpsimd.tensor_tensor(low, raw[:, i % 2, :], high.bitcast(F32),
                                        ALU.subtract).then_inc(pool_split, 1)

            for i in range(NSTART, FIRST_W + 6):
                split(i)
            for s in range(KH * NC + 1):
                if s >= 1:
                    ff_pool_sum(pool, s - 1)
                if s < KH * NC:
                    ff_pool_diff(pool, s)
            for i in range(FIRST_W + 6, FIRST_W + W_MOE + 4):
                split(i)
            for e in range(E):
                for c in range(NC):
                    if c == 0 and e >= 1 and e + 1 < E:
                        for i in (2, 3):
                            split(FIRST_W + W_MOE + 2 * e + i)
                    for dc in range(KD):
                        moe_add(pool, e, c, dc)

        def split_products(pe, psum, w, xs, n, last_sem=None):
            k = 0
            for i in range(n):
                (wh, wl), (xh, xl) = w(i), xs(i)
                for a, b in ((wh, xh), (wh, xl), (wl, xh)):
                    mm = pe.matmul(psum, a, b, start=(k == 0), stop=(k == 3 * n - 1))
                    k += 1
            if last_sem is not None:
                mm.then_inc(last_sem, 1)

        @block.tensor
        def _(pe):
            def hidden(slot, kk, a, w):
                return [hid[:, slot, k, kk * CW + a:kk * CW + a + w] for k in range(2)]

            def normed(kk, sl):
                return [xn[:, k, kk, sl] for k in range(2)]

            pe.wait_ge(*piece_split(0))
            for c, (a, w) in enumerate(CHUNKS):
                pe.wait_ge(*piece_split(1 + c))
                for dc in range(KD):
                    if c >= 1:
                        pe.wait_ge(h_set, KD * (c - 1) + dc + 1)
                    wl = [wslot[:, WSLOTS - 1, k, 0:KF * D].rearrange("p (a n) -> p a n", n=D) for k in range(2)]
                    split_products(pe, BD[dc][:, 0:w],
                                   lambda i: [t[:, i, dc * P:(dc + 1) * P] for t in wl],
                                   lambda i: [hid[:, c % 2, k, i * w:(i + 1) * w] for k in range(2)],
                                   KF, emb_mm)

            def layernorm(n, source, per):
                if n == 0:
                    pe.wait_ge(consts, 1)

                def variance(c):
                    a, w = CHUNKS[c]
                    pe.wait_ge(ln_sq[n], c + 1)
                    if c >= 2:
                        pe.wait_ge(ln_rs[n], c - 1)
                    for k in range(KD):
                        mm = pe.matmul(BT[c % 2][:, 0:w], mean_w[:, :], sq[:, k, 0:w],
                                       start=(k == 0), stop=(k == KD - 1))
                    mm.then_inc(ln_var[n], 1)

                for c, (a, w) in enumerate(CHUNKS):
                    pe.wait_ge(source, per * (c + 1))
                    if c >= 2:
                        pe.wait_ge(ln_xc[n], c - 1)
                    for k in range(KD):
                        mm = pe.matmul(BS[c % 2][:, 0:w], mean_w[:, :], h[:, k, a:a + w],
                                       start=(k == 0), stop=(k == KD - 1))
                    mm.then_inc(ln_mean[n], 1)
                    if c >= 1:
                        variance(c - 1)
                variance(NC - 1)

            def attention(l, n):
                q_w, k_w, v_w, o_w = (W_QKVO[l] + i for i in range(4))

                def project_qk(c):
                    a, w = CHUNKS[c]
                    pe.wait_ge(ln_out[n], c + 1)
                    for m in range(2 * KO):
                        j = 2 * KO * c + m
                        wj = (q_w, k_w)[m // KO]
                        if c == 0 and m % KO == 0:
                            wait_weight(pe, wj)
                        if j >= 2:
                            pe.wait_ge((qk_act, qk_dve)[j % 2][l], j // 2)
                        if m < 2 and c >= 1:
                            pe.wait_ge(h_attn[l], KD * (c - 1) + m + 1)
                        mc = m % KO
                        split_products(pe, BD[m % 2][:, 0:w],
                                       lambda i: [weight(wj, k, HD)[:, i, mc * P:(mc + 1) * P] for k in range(2)],
                                       lambda i: normed(i, slice(a, a + w)), KD, qk_mm[l])

                def project_v(g):
                    if g == 0:
                        wait_weight(pe, v_w)
                    c = g // GC
                    for half in range(2):
                        if g % GC == 0:
                            pe.wait_ge((qk_act, qk_dve)[half][l], KO * (c + 1))
                        else:
                            pe.wait_ge((v_act, v_dve)[half][l], g)
                        split_products(pe, BD[half][0:NTOK[g], :],
                                       lambda i: normed(i, cols(g)),
                                       lambda i: [weight(v_w, k, HD)[:, i, half * 512:(half + 1) * 512]
                                                  for k in range(2)], KD, v_mm[l])

                def scores(q):
                    c, g, t = QUADS[q]
                    nt, a = NTOK[g], g * GW - CHUNKS[c][0]
                    if t == 0 and g % GC == 0:
                        pe.wait_ge(qk_act[l], KO * (c + 1))
                        pe.wait_ge(qk_dve[l], KO * (c + 1))
                    if q >= 2:
                        pe.wait_ge(s_exp[l], QH * (q - 1))
                    bank4 = BS[q % 2][0:nt, 0:QH * GW].rearrange("p (h n) -> p h n", h=QH)[:, :, 0:nt]
                    pe.matmul(bank4, identb[0:nt, 0:nt], maskb[0:nt, l, :, 0:nt], start=True, stop=False,
                              skip_group_check=True)
                    r = DH * (t % 2)
                    for i, hd in enumerate(heads(t)):
                        mm = pe.matmul(BS[q % 2][0:nt, i * GW:i * GW + nt],
                                       work[r:r + DH, hd // 2, a:a + nt], work[r:r + DH, KO + hd // 2, a:a + nt],
                                       start=False, stop=(i == QH - 1), skip_group_check=True)
                    mm.then_inc(s_mm[l], 1)

                def transposes(q):
                    c, g, t = QUADS[q]
                    nt = NTOK[g]
                    pe.wait_ge(p_norm[l], q + 1)
                    if q >= 2:
                        pe.wait_ge(t_dve[l], q - 1)
                    for i in range(QH):
                        mm = pe.transpose(BT[q % 2][0:nt, i * GW:i * GW + nt],
                                          probs[0:nt, q % 3, i * GW:i * GW + nt], ident[0:nt, 0:nt])
                    mm.then_inc(t_mm[l], 1)

                def values(q):
                    c, g, t = QUADS[q]
                    nt = NTOK[g]
                    pe.wait_ge(t_dve[l], q + 1)
                    if t == 0:
                        pe.wait_ge(v_act[l], g + 1)
                        pe.wait_ge(v_dve[l], g + 1)
                    if q >= 4:
                        pe.wait_ge(o_low[l], q // 2 - 1)
                    r = DH * (t % 2)
                    for i, hd in enumerate(heads(t)):
                        mm = pe.matmul(BO[q // 2 % 2][r:r + DH, i * GW:i * GW + nt],
                                       vbuf[0:nt, g % 2, hd * DH:(hd + 1) * DH],
                                       probsT[0:nt, q % 2, i * GW:i * GW + nt], start=True, stop=True,
                                       skip_group_check=True)
                    mm.then_inc(o_mm[l], 1)

                def project_out(c):
                    a, w = CHUNKS[c]
                    if c == 0:
                        wait_weight(pe, o_w)
                    pe.wait_ge(o_low[l], NQ // 2 * (GROUPS[c][-1] + 1))
                    for dc in range(KD):
                        pe.wait_ge((v_act, v_dve)[dc][l], GROUPS[c][-1] + 1)
                        split_products(pe, BD[dc][:, 0:w],
                                       lambda i: [weight(o_w, k, D)[:, i, dc * P:(dc + 1) * P] for k in range(2)],
                                       lambda i: hidden(c % 2, i, 0, w), KO, out_mm[l])

                for c in range(NC):
                    project_qk(c)
                    mine = [q for q in range(len(QUADS)) if QUADS[q][0] == c]
                    for q in mine + [mine[-1] + 1, mine[-1] + 2, mine[-1] + 3]:
                        if q in mine and QUADS[q][2] == 0:
                            project_v(QUADS[q][1])
                        if q in mine:
                            scores(q)
                        if q - 2 in mine:
                            transposes(q - 2)
                        if q - 3 in mine:
                            values(q - 3)
                    project_out(c)

            layernorm(0, h_set, KD)
            pe.wait_ge(masks, 2)
            attention(0, 0)
            layernorm(1, h_attn[0], KD)

            def ff_up(c):
                a, w = CHUNKS[c]
                pe.wait_ge(ln_out[1], c + 1)
                if c == 0:
                    wait_weight(pe, W_FF)
                for m in range(KH):
                    s = KH * c + m
                    if s >= 4:
                        pe.wait_ge(ff_t, s - 3)
                    split_products(pe, BH[s % 4][:, 0:w],
                                   lambda i: [weight(W_FF, k, FF)[:, i, m * P:(m + 1) * P] for k in range(2)],
                                   lambda i: normed(i, slice(a, a + w)), KD, ff1_mm)

            def ff_down(c):
                a, w = CHUNKS[c]
                pe.wait_ge(ff_hid, KH * (c + 1))
                if c == 0:
                    wait_weight(pe, W_FF + 1)
                for dc in range(KD):
                    if c >= 1:
                        pe.wait_ge(ff2_ev, KD * (c - 1) + dc + 1)
                    split_products(pe, BO[dc][:, 0:w],
                                   lambda i: [weight(W_FF + 1, k, D)[:, i, dc * P:(dc + 1) * P] for k in range(2)],
                                   lambda i: hidden(c % 2, i, 0, w), KH, ff2_mm)

            for c in range(NC):
                ff_up(c)
                if c >= 1:
                    ff_down(c - 1)
            ff_down(NC - 1)
            layernorm(2, h_ff, KD)
            attention(1, 2)
            layernorm(3, h_attn[1], KD)

            pe.wait_ge(params, 5)
            for g in range(NG):
                pe.wait_ge(ln_out[3], g // GC + 1)
                split_products(pe, BO[0][0:NTOK[g], g * E:(g + 1) * E],
                               lambda i: normed(i, cols(g)),
                               lambda i: [gateR[:, k, i * E:(i + 1) * E] for k in range(2)], KD,
                               log_mm)

            def sum_counts(i):
                pe.wait_ge(cnt_ready, i + 1)
                pe.matmul(BT[1][:, 0:1], mean_w[:, :], count[:, i % 2:i % 2 + 1], start=True,
                          stop=True).then_inc(cnt_mm, 1)

            def moe_up(e, c):
                a, w = CHUNKS[c]
                if c == 0:
                    wait_weight(pe, W_MOE + 2 * e)
                for m in range(KH):
                    s = (e * NC + c) * KH + m
                    if s >= 4:
                        pe.wait_ge(m_gelu, s - 3)
                    split_products(pe, BH[s % 4][:, 0:w],
                                   lambda i: [weight(W_MOE + 2 * e, k, FF)[:, i, m * P:(m + 1) * P] for k in range(2)],
                                   lambda i: normed(i, slice(a, a + w)), KD, m1_mm)
                    if s < 16:
                        sum_counts(2 * s)
                        sum_counts(2 * s + 1)

            def spread_gates(e):
                for c, (a, w) in enumerate(CHUNKS):
                    j = e * NC + c
                    if j >= 2:
                        pe.wait_ge(gb_act, j - 1)
                    for g in GROUPS[c]:
                        wd = min(GW, w - (g * GW - a))
                        nt = NTOK[g]
                        mm = pe.matmul(BT[j % 2][:, g * GW - a:g * GW - a + wd],
                                       gates[0:nt, g * E + e:g * E + e + 1].to_broadcast([nt, P]),
                                       ident[0:nt, 0:wd], start=True, stop=True)
                    mm.then_inc(gb_mm, 1)

            def moe_down(e, c):
                a, w = CHUNKS[c]
                j = e * NC + c
                pe.wait_ge(m_hid, KH * (j + 1))
                if c == 0:
                    wait_weight(pe, W_MOE + 2 * e + 1)
                for dc in range(KD):
                    if j >= 1:
                        pe.wait_ge(m_y, KD * (j - 1) + dc + 1)
                    split_products(pe, BO[dc][:, 0:w],
                                   lambda i: [weight(W_MOE + 2 * e + 1, k, D)[:, i, dc * P:(dc + 1) * P]
                                              for k in range(2)],
                                   lambda i: hidden(j % 2, i, 0, w), KH, m2_mm)

            steps = [(e, c) for e in range(E) for c in range(NC)]
            for n, (e, c) in enumerate(steps):
                moe_up(e, c)
                if n == 1:
                    pe.wait_ge(gates_ready, 1)
                    spread_gates(0)
                if c == 1 and e >= 1:
                    spread_gates(e)
                if n >= 1:
                    moe_down(*steps[n - 1])
            moe_down(*steps[-1])

        @block.scalar
        def _(act):
            done = [0]

            def link(ins):
                done[0] += 1
                ins.then_inc(act_line, 1)
                act.wait_ge(act_line, done[0])

            def high_part(i):
                act.wait_ge(raw_in[i % 2], 16 * (i // 2 + 1))
                if place_free(i):
                    act.wait_ge(*place_free(i))
                nc.scalar.activation(piece_place(i)[0], raw[:, i % 2, 0:piece_size(i)],
                                     ACT.Copy).then_inc(high_ready, 1)

            for i in range(FIRST_W):
                high_part(i)
            act.wait_ge(consts, 7)
            act.wait_ge(small_in, 16)

            def layernorm(n):
                def square(c):
                    w = CHUNKS[c][1]
                    act.wait_ge(ln_xc[n], c + 1)
                    if c >= 1:
                        act.wait_ge(ln_var[n], c)
                    nc.scalar.activation(sq[:, :, 0:w], xc[:, c % 2, :, 0:w], ACT.Square).then_inc(ln_sq[n], 1)

                square(0)
                for c, (a, w) in enumerate(CHUNKS):
                    act.wait_ge(ln_var[n], c + 1)
                    if c >= 1:
                        act.wait_ge(ln_out[n], c)
                    nc.scalar.activation(rt[:, 0:w], BT[c % 2][:, 0:w], ACT.Ln,
                                         bias=c_eps[:, 0:1]).then_inc(ln_ln[n], 1)
                    act.wait_ge(ln_ln[n], c + 1)
                    nc.scalar.activation(rs[:, 0:w], rt[:, 0:w], ACT.Exp, scale=-0.5).then_inc(ln_rs[n], 1)
                    if c + 1 < NC:
                        square(c + 1)

            def attention(l):
                def move_q(c):
                    w = CHUNKS[c][1]
                    for m in range(0, 2 * KO, 2):
                        act.wait_ge(qk_mm[l], 2 * KO * c + m + 1)
                        nc.scalar.activation(work[:, m, 0:w], BD[0][:, 0:w], ACT.Copy).then_inc(qk_act[l], 1)

                def move_v(g):
                    act.wait_ge(v_mm[l], 2 * g + 1)
                    if g >= 2:
                        act.wait_ge(o_mm[l], NQ * (g - 1))
                    nc.scalar.activation(vbuf[0:NTOK[g], g % 2, 0:512], BD[0][0:NTOK[g], :],
                                         ACT.Copy).then_inc(v_act[l], 1)

                def exps(q):
                    c, g, t = QUADS[q]
                    nt = NTOK[g]
                    act.wait_ge(s_max[l], q + 1)
                    if q >= 3:
                        act.wait_ge(t_mm[l], q - 2)
                    for i in range(QH):
                        k = QH * (q % 4) + i
                        nc.scalar.activation(probs[0:nt, q % 3, i * GW:i * GW + nt],
                                             BS[q % 2][0:nt, i * GW:i * GW + nt], ACT.Exp,
                                             bias=negmax[0:nt, k:k + 1], scale=DH ** -0.5,
                                             accum_out=sums[0:nt, k:k + 1]).then_inc(s_exp[l], 1)

                def high_out(pair):
                    c, g, t = QUADS[2 * pair]
                    nt, a = NTOK[g], g * GW - CHUNKS[c][0]
                    act.wait_ge(o_mm[l], 2 * pair + 2)
                    if c >= 2:
                        act.wait_ge(out_mm[l], KD * (c - 1))
                    nc.scalar.activation(heads_out(0, c, t, a, nt), out_pair(pair, nt),
                                         ACT.Copy).then_inc(o_high[l], 1)

                for c in range(NC):
                    move_q(c)
                    mine = [q for q in range(len(QUADS)) if QUADS[q][0] == c]
                    for q in mine + [mine[-1] + 1, mine[-1] + 2, mine[-1] + 3]:
                        if q in mine and QUADS[q][2] == 0:
                            move_v(QUADS[q][1])
                        if q in mine:
                            exps(q)
                        if q - 3 in mine and q % 2 == 0:
                            high_out((q - 3) // 2)

            layernorm(0)
            for i in range(FIRST_W, NSTART):
                high_part(i)
            attention(0)
            layernorm(1)

            def ff_load(s):
                v, a, kn, y0, y1 = ff_bufs(s)
                act.wait_ge(ff1_mm, s + 1)
                if s >= 3:
                    act.wait_ge(ff_sum, s - 2)
                nc.scalar.activation(v, BH[s % 4][:, 0:CHUNKS[s // KH][1]], ACT.Identity,
                                     bias=b1u[:, s % KH:s % KH + 1], scale=UNIT).then_inc(ff_t, 1)

            def ff_shape(s):
                v, a, kn, y0, y1 = ff_bufs(s)
                act.wait_ge(ff_v, s + 1)
                if s >= 3:
                    act.wait_ge(ff_hid, s - 2)
                nc.scalar.activation(a, v, ACT.Abs).then_inc(ff_abs, 1)
                act.wait_ge(ff_abs, s + 1)
                nc.scalar.activation(v, v, ACT.Relu, scale=0.25).then_inc(ff_relu, 1)

            def ff_knots(s):
                v, a, kn, y0, y1 = ff_bufs(s)
                act.wait_ge(ff_knot, s + 1)
                nc.scalar.activation(y0, kn, ACT.Gelu, scale=-1.0 / UNIT).then_inc(ff_y0, 1)
                nc.scalar.activation(y1, kn, ACT.Gelu, bias=c_knot[:, 0:1], scale=-1.0 / UNIT).then_inc(ff_y1, 1)

            NS = KH * NC
            ff_load(0)
            for s in range(NS):
                ff_shape(s)
                if s + 1 < NS:
                    ff_load(s + 1)
                ff_knots(s)
            layernorm(2)
            attention(1)
            layernorm(3)

            def spread(e):
                for c, (a, w) in enumerate(CHUNKS):
                    j = e * NC + c
                    act.wait_ge(gb_mm, j + 1)
                    if e >= 2:
                        act.wait_ge(m_y, KD * ((e - 2) * NC + c + 1))
                    nc.scalar.activation(moe_gate(e, c)[:, 0:w], BT[j % 2][:, 0:w], ACT.Copy).then_inc(gb_act, 1)

            for s in range(E * NC * KH):
                e, c, m = s // (NC * KH), s // KH % NC, s % KH
                w = CHUNKS[c][1]
                act.wait_ge(m1_mm, s + 1)
                if s >= 4:
                    act.wait_ge(m_hid, s - 3)
                nc.scalar.activation(moe_g(s)[:, 0:w], BH[s % 4][:, 0:w], ACT.Gelu_apprx_tanh,
                                     bias=prm[:, S_B1M + e * KH + m:S_B1M + e * KH + m + 1]).then_inc(m_gelu, 1)
                if c == 1 and m == KH - 1:
                    spread(e)

        @block.vector
        def _(dve):
            done = [0]

            def tick(ins):
                done[0] += 1
                ins.then_inc(dve_line, 1)
                return done[0]

            def link(ins):
                dve.wait_ge(dve_line, tick(ins))

            dve.wait_ge(small_in, 16)
            pos = prm[:, S_POS:S_CLS].rearrange("p (k n) -> p k n", k=KD)
            for k in range(KD):
                nc.vector.tensor_scalar(addT[:, k, 1:TOK], pos[:, k, 1:TOK], prm[:, S_BLIN + k:S_BLIN + k + 1],
                                        None, ALU.add).then_inc(params, 1)
            nc.vector.tensor_tensor(addT[:, :, 0], pos[:, :, 0], prm[:, S_CLS:S_BLIN], ALU.add).then_inc(params, 1)
            tick(nc.vector.tensor_scalar(b1u[:, :], prm[:, S_B1F:S_B2F], UNIT, None, ALU.mult))
            tick(nc.vector.tensor_scalar(b2u[:, :], prm[:, S_B2F:S_B1M], UNIT, None, ALU.mult))
            nc.vector.tensor_copy(gateR[:, 0, :], prm[:, S_GATE:S_END]).then_inc(params, 1)
            dve.wait_ge(params, 4)
            nc.vector.tensor_tensor(gateR[:, 1, :], prm[:, S_GATE:S_END], gateR[:, 0, :].bitcast(F32),
                                    ALU.subtract).then_inc(params, 1)
            nc.vector.memset(h[:, :, 0:(NG - 1) * GW].rearrange("p k (g n) -> p k g n", n=GW)[:, :, :, GW - 1:GW],
                             0.0).then_inc(pads, 1)

            def low_part(i):
                dve.wait_ge(high_ready, i + 1)
                high, low = piece_place(i)
                nc.vector.tensor_tensor(low, raw[:, i % 2, 0:piece_size(i)], high.bitcast(F32),
                                        ALU.subtract).then_inc(start_split, 1)

            def set_h(c):
                for dc in range(KD):
                    dve.wait_ge(emb_mm, KD * c + dc + 1)
                    for g in GROUPS[c]:
                        ni = NTOK[g] // TOK
                        a = g * GW - CHUNKS[c][0]
                        ins = nc.vector.tensor_tensor(
                            h[:, dc, cols(g)].rearrange("p (i n) -> p i n", n=TOK),
                            BD[dc][:, a:a + NTOK[g]].rearrange("p (i n) -> p i n", n=TOK),
                            addT[:, dc:dc + 1, :].to_broadcast([P, ni, TOK]), ALU.add)
                    ins.then_inc(h_set, 1)

            low_part(0)
            low_part(1)
            dve.wait_ge(params, 3)
            for c in range(NC):
                if c + 2 < FIRST_W:
                    low_part(c + 2)
                set_h(c)
            dve.wait_ge(mats_in, 32)
            nc.vector.tensor_copy(identb[:, :], ident[:, :]).then_inc(masks, 1)
            for l in range(2):
                for i in range(QH):
                    ins = nc.vector.tensor_copy(maskb[:, l, i, :], maskf[:, l, :])
            ins.then_inc(masks, 1)
            dve.wait_ge(emb_mm, KD * NC)
            nc.vector.memset(hid[:, :, :, :].rearrange("p s k (m n) -> p (s k m) n", n=GW)[:, :, GW - 1:GW].bitcast(F32),
                             0.0).then_inc(pads, 1)

            def layernorm(n):
                def center(c):
                    a, w = CHUNKS[c]
                    dve.wait_ge(ln_mean[n], c + 1)
                    if c >= 2:
                        dve.wait_ge(ln_out[n], c - 1)
                    mean = BS[c % 2][:, 0:w].rearrange("p (a n) -> p a n", a=1).to_broadcast([P, KD, w])
                    nc.vector.tensor_tensor(xc[:, c % 2, :, 0:w], h[:, :, a:a + w], mean,
                                            ALU.subtract).then_inc(ln_xc[n], 1)

                center(0)
                for c, (a, w) in enumerate(CHUNKS):
                    if c + 1 < NC:
                        center(c + 1)
                    dve.wait_ge(ln_rs[n], c + 1)
                    r, t = rs[:, 0:w], rt[:, 0:w]
                    link(nc.vector.tensor_tensor(t, r, r, ALU.mult))
                    link(nc.vector.scalar_tensor_tensor(t, BT[c % 2][:, 0:w], EPS, t, ALU.add, ALU.mult))
                    link(nc.vector.tensor_scalar(t, t, -0.5, 1.5, ALU.mult, ALU.add))
                    link(nc.vector.tensor_tensor(r, t, r, ALU.mult))
                    x2 = xc[:, c % 2, :, 0:w]
                    rb = rs[:, 0:w].rearrange("p (a n) -> p a n", a=1).to_broadcast([P, KD, w])
                    link(nc.vector.tensor_tensor(x2, x2, rb, ALU.mult))
                    link(nc.vector.tensor_copy(xn[:, 0, :, a:a + w], x2))
                    nc.vector.tensor_tensor(xn[:, 1, :, a:a + w], x2, xn[:, 0, :, a:a + w].bitcast(F32),
                                            ALU.subtract).then_inc(ln_out[n], 1)

            def attention(l):
                def move_k(c):
                    w = CHUNKS[c][1]
                    for m in range(1, 2 * KO, 2):
                        dve.wait_ge(qk_mm[l], 2 * KO * c + m + 1)
                        nc.vector.tensor_copy(work[:, m, 0:w], BD[1][:, 0:w]).then_inc(qk_dve[l], 1)

                def move_v(g):
                    dve.wait_ge(v_mm[l], 2 * g + 2)
                    if g >= 2:
                        dve.wait_ge(o_mm[l], NQ * (g - 1))
                    nc.vector.tensor_copy(vbuf[0:NTOK[g], g % 2, 512:HD], BD[1][0:NTOK[g], :]).then_inc(v_dve[l], 1)

                def row_max(q):
                    c, g, t = QUADS[q]
                    nt = NTOK[g]
                    dve.wait_ge(s_mm[l], q + 1)
                    k = QH * (q % 4)
                    link(nc.vector.tensor_reduce(
                        maxes[0:nt, k:k + QH],
                        BS[q % 2][0:nt, 0:QH * GW].rearrange("p (h n) -> p h n", h=QH)[:, :, 0:nt], AX_X, ALU.max))
                    nc.vector.tensor_scalar(negmax[0:nt, k:k + QH], maxes[0:nt, k:k + QH], -DH ** -0.5, None,
                                            ALU.mult).then_inc(s_max[l], 1)

                def normalise(q):
                    c, g, t = QUADS[q]
                    nt, k = NTOK[g], QH * (q % 4)
                    dve.wait_ge(s_exp[l], QH * (q + 1))
                    link(nc.vector.reciprocal(rsum[0:nt, k:k + QH], sums[0:nt, k:k + QH]))
                    pr = probs[0:nt, q % 3, :].rearrange("p (h n) -> p h n", h=QH)[:, :, 0:nt]
                    rb = rsum[0:nt, k:k + QH].rearrange("p (h n) -> p h n", n=1).to_broadcast([nt, QH, nt])
                    nc.vector.tensor_tensor(pr, pr, rb, ALU.mult).then_inc(p_norm[l], 1)

                def move_t(q):
                    c, g, t = QUADS[q]
                    nt = NTOK[g]
                    dve.wait_ge(t_mm[l], q + 1)
                    if q >= 2:
                        dve.wait_ge(o_mm[l], q - 1)
                    nc.vector.tensor_copy(
                        probsT[0:nt, q % 2, :].rearrange("p (h n) -> p h n", h=QH)[:, :, 0:nt],
                        BT[q % 2][0:nt, 0:QH * GW].rearrange("p (h n) -> p h n", h=QH)[:, :, 0:nt],
                    ).then_inc(t_dve[l], 1)

                def low_out(pair):
                    c, g, t = QUADS[2 * pair]
                    nt, a = NTOK[g], g * GW - CHUNKS[c][0]
                    dve.wait_ge(o_high[l], pair + 1)
                    nc.vector.tensor_tensor(heads_out(1, c, t, a, nt), out_pair(pair, nt),
                                            heads_out(0, c, t, a, nt).bitcast(F32),
                                            ALU.subtract).then_inc(o_low[l], 1)

                def add_out(c):
                    a, w = CHUNKS[c]
                    for dc in range(KD):
                        dve.wait_ge(out_mm[l], KD * c + dc + 1)
                        if l == 0:
                            ins = nc.vector.tensor_tensor(h[:, dc, a:a + w], BD[dc][:, 0:w], h[:, dc, a:a + w],
                                                          ALU.add)
                        else:
                            ins = nc.vector.scalar_tensor_tensor(
                                h[:, dc, a:a + w], BD[dc][:, 0:w], prm[:, S_BO + dc:S_BO + dc + 1],
                                h[:, dc, a:a + w], ALU.add, ALU.add)
                        ins.then_inc(h_attn[l], 1)

                for c in range(NC):
                    move_k(c)
                    mine = [q for q in range(len(QUADS)) if QUADS[q][0] == c]
                    for q in mine + [mine[-1] + 1, mine[-1] + 2, mine[-1] + 3]:
                        if q in mine and QUADS[q][2] == 0:
                            move_v(QUADS[q][1])
                        if q in mine:
                            row_max(q)
                        if q - 1 in mine:
                            normalise(q - 1)
                        if q - 2 in mine:
                            move_t(q - 2)
                        if q - 3 in mine and q % 2 == 0:
                            low_out((q - 3) // 2)
                    add_out(c)

            layernorm(0)
            for i in range(FIRST_W, NSTART):
                low_part(i)
            attention(0)
            layernorm(1)

            NS = KH * NC

            def ff_round(s):
                v = ff_bufs(s)[0]
                dve.wait_ge(ff_t, s + 1)
                nc.vector.tensor_scalar(v, v, MAGIC, MAGIC, ALU.add, ALU.subtract).then_inc(ff_v, 1)

            def ff_find(s):
                v, a, kn, y0, y1 = ff_bufs(s)
                dve.wait_ge(ff_abs, s + 1)
                link(nc.vector.tensor_scalar(a, a, 16 * KNOT, (KNOT - 1) / 2, ALU.min, ALU.subtract))
                nc.vector.tensor_scalar(kn, a, MAGIC_KNOT, MAGIC_KNOT, ALU.add, ALU.subtract).then_inc(ff_knot, 1)
                dve.wait_ge(ff_knot, s + 1)
                nc.vector.tensor_tensor(a, kn, a, ALU.subtract).then_inc(ff_frac, 1)

            def ff_interp(s):
                v, a, kn, y0, y1 = ff_bufs(s)
                dve.wait_ge(ff_dy, s + 1)
                dve.wait_ge(ff_frac, s + 1)
                nc.vector.scalar_tensor_tensor(a, a, -(KNOT - 1) / 2, y1, ALU.add, ALU.mult).then_inc(ff_lin, 1)
                dve.wait_ge(ff_lin, s + 1)
                nc.vector.scalar_tensor_tensor(y0, y0, KNOT, a, ALU.mult, ALU.subtract).then_inc(ff_q, 1)

            def ff_store(s):
                v, a, kn, y0, y1 = ff_bufs(s)
                c, m = s // KH, s % KH
                w = CHUNKS[c][1]
                dve.wait_ge(ff_sum, s + 1)
                link(nc.vector.tensor_scalar(y0, y0, UNIT / KNOT, MAGIC, ALU.mult, ALU.add))
                if c >= 2:
                    dve.wait_ge(ff2_mm, KD * (c - 1))
                high, low = (hid[:, c % 2, k, m * CW:m * CW + w] for k in range(2))
                link(nc.vector.tensor_scalar(high, y0, MAGIC, None, ALU.subtract))
                nc.vector.scalar_tensor_tensor(low, y0, MAGIC, high.bitcast(F32), ALU.subtract,
                                               ALU.subtract).then_inc(ff_hid, 1)

            def ff_out(c):
                a, w = CHUNKS[c]
                for dc in range(KD):
                    dve.wait_ge(ff2_mm, KD * c + dc + 1)
                    t = rt[:, 0:w]
                    nc.vector.tensor_scalar(t, BO[dc][:, 0:w], b2u[:, dc:dc + 1], MAGIC, ALU.add,
                                            ALU.add).then_inc(ff2_ev, 1)
                    dve.wait_ge(ff2_ev, KD * c + dc + 1)
                    link(nc.vector.tensor_scalar(t, t, MAGIC, 1.0 / UNIT, ALU.subtract, ALU.mult))
                    nc.vector.tensor_tensor(h[:, dc, a:a + w], h[:, dc, a:a + w], t, ALU.add).then_inc(h_ff, 1)
                    dve.wait_ge(h_ff, KD * c + dc + 1)

            for s in range(NS + 1):
                if s < NS:
                    ff_round(s)
                if s >= 1:
                    ff_interp(s - 1)
                if s < NS:
                    ff_find(s)
                if s >= 1:
                    ff_store(s - 1)
                if s >= 2 * KH and s % KH == 2:
                    ff_out(s // KH - 2)
            ff_out(NC - 2)
            ff_out(NC - 1)
            layernorm(2)
            attention(1)
            layernorm(3)

            full = (NG - 1) * E
            dve.wait_ge(log_mm, NG)
            dve.wait_ge(consts, 7)
            link(nc.vector.tensor_copy(logits[0:NTOK[0], 0:full], BO[0][0:NTOK[0], 0:full]))
            link(nc.vector.tensor_copy(logits[0:NTOK[-1], full:], BO[0][0:NTOK[-1], full:NG * E]))
            link(nc.vector.memset(found[:, :], 0))

            def search(i):
                if i > 0:
                    bit = 31 - i
                    link(nc.vector.tensor_scalar(tryb[:, :], found[:, :], 1 << bit, None, ALU.bitwise_or))
                src, than = (logits, 0.0) if i == 0 else (keys, tryb[:, 0:1].bitcast(F32))
                nc.vector.tensor_scalar(below[:, :], src[:, :], than, None, ALU.is_lt, ALU.add,
                                        accum_out=count[:, i % 2:i % 2 + 1]).then_inc(cnt_ready, 1)
                dve.wait_ge(cnt_mm, i + 1)
                total = BT[1][:, 0:1]
                if i == 0:
                    link(nc.vector.tensor_scalar(sign[:, :], total, TOPK / D, -2.0, ALU.is_ge, ALU.mult))
                    link(nc.vector.tensor_scalar(sign[:, :], sign[:, :], 1.0, None, ALU.add))
                    link(nc.vector.tensor_scalar(rank[:, :], sign[:, :], (2 * TOPK - NLOG - 1) / (2 * D),
                                                 (NLOG + 1) / (2 * D), ALU.mult, ALU.add))
                    for rows, a, b in ((NTOK[0], 0, full), (NTOK[-1], full, NG * E)):
                        link(nc.vector.tensor_scalar(keys[0:rows, a:b], logits[0:rows, a:b], sign[0:rows, 0:1],
                                                     None, ALU.mult))
                else:
                    link(nc.vector.tensor_scalar(newb[:, :], total, rank[:, 0:1], float(1 << bit), ALU.is_lt,
                                                 ALU.mult))
                    link(nc.vector.tensor_tensor(found[:, :], found[:, :], newb[:, :], ALU.bitwise_or))

            def gate():
                link(nc.vector.tensor_scalar(kth[:, :], found[:, :].bitcast(F32), sign[:, 0:1], None, ALU.mult))
                link(nc.vector.scalar_tensor_tensor(gates[0:NTOK[0], 0:full], logits[0:NTOK[0], 0:full],
                                                    kth[0:NTOK[0], 0:1], logits[0:NTOK[0], 0:full],
                                                    ALU.is_ge, ALU.mult))
                nc.vector.scalar_tensor_tensor(gates[0:NTOK[-1], full:], logits[0:NTOK[-1], full:],
                                               kth[0:NTOK[-1], 0:1], logits[0:NTOK[-1], full:],
                                               ALU.is_ge, ALU.mult).then_inc(gates_ready, 1)

            def moe_split(s):
                c, m = s // KH % NC, s % KH
                w = CHUNKS[c][1]
                j = s // KH
                dve.wait_ge(m_gelu, s + 1)
                if j >= 2:
                    dve.wait_ge(m2_mm, KD * (j - 1))
                high, low = (hid[:, j % 2, k, m * CW:m * CW + w] for k in range(2))
                nc.vector.tensor_copy(high, moe_g(s)[:, 0:w]).then_inc(m_high, 1)
                dve.wait_ge(m_high, s + 1)
                nc.vector.tensor_tensor(low, moe_g(s)[:, 0:w], high.bitcast(F32), ALU.subtract).then_inc(m_hid, 1)

            def moe_out(e, c):
                w = CHUNKS[c][1]
                for dc in range(KD):
                    j = (e * NC + c) * KD + dc
                    dve.wait_ge(m2_mm, j + 1)
                    dve.wait_ge(gb_act, e * NC + c + 1)
                    if j >= 4:
                        dve.wait_ge(h_moe, j - 3)
                    nc.vector.scalar_tensor_tensor(
                        moe_y(j)[:, 0:w], BO[dc][:, 0:w], prm[:, S_B2M + dc * E + e:S_B2M + dc * E + e + 1],
                        moe_gate(e, c)[:, 0:w], ALU.add, ALU.mult).then_inc(m_y, 1)

            steps = [(e, c) for e in range(E) for c in range(NC)]
            for s in range(E * NC * KH):
                if s < 16:
                    search(2 * s)
                    search(2 * s + 1)
                if s == 15:
                    gate()
                moe_split(s)
                if s % KH == 4 and s >= 2 * KH:
                    moe_out(*steps[s // KH - 2])
            moe_out(*steps[-2])
            moe_out(*steps[-1])


def layout(i):
    import numpy as np

    def rows(a):
        k = a.shape[0] // P
        return a.reshape(k, P, -1).transpose(1, 0, 2).reshape(P, -1)

    i = {k: np.asarray(v) for k, v in i.items()}
    col = np.array([g * GW + t for g in range(NG) for t in range(NTOK[g])])
    patch = np.array([c for n, c in enumerate(col) if n % TOK])
    px = i["x"].reshape(B, C, SIDE, PATCH, SIDE, PATCH).transpose(1, 3, 5, 0, 2, 4).reshape(C * PATCH * PATCH, -1)
    xt = np.zeros((C * PATCH * PATCH, T), np.float32)
    xt[:, patch] = px
    a = {"x": xt.reshape(KF, P, T).transpose(1, 0, 2), "w_lin": rows(i["L0_tok_W_lin"].T)}
    a["attn0"] = np.stack([rows(i[f"L0_attn_w{n}"].reshape(HD, D).T) for n in "qkv"]
                          + [rows(i["L0_attn_wo"].T)])
    a["ffn"] = np.stack([rows(i["L0_ffn_w1"]), rows(i["L0_ffn_w2"])])
    a["attn1"] = np.stack([rows(i[f"L1_attn_W{n}"]) for n in "qkvo"])
    w1, w2 = i["L1_ffn_w1"], i["L1_ffn_w2"]
    a["moe"] = np.stack([rows(w.T) for e in range(E) for w in (w1[e], w2[e])])
    a["small"] = np.concatenate(
        [rows(i["L0_tok_position_embeddings"][0].T)]
        + [rows(v.reshape(-1, 1)) for v in (i["L0_tok_class_token"], i["L0_tok_b_lin"], i["L1_attn_bo"],
                                            i["L0_ffn_b1"], i["L0_ffn_b2"])]
        + [rows(i["L1_ffn_b1"][e].reshape(-1, 1)) for e in range(E)]
        + [rows(i["L1_ffn_b2"].T), rows(i["L1_ffn_gate_weight"].T)], axis=1)
    t = np.arange(P)
    same = (t[:, None] // TOK == t[None, :] // TOK)[:, :GW]
    late = (t[None, :] > t[:, None])[:, :GW]
    a["ident"] = np.eye(P, dtype=np.float32)
    a["mask"] = np.stack([np.where(same & ~late, 0.0, -1e30), np.where(same, 0.0, -1e30)],
                         axis=1).astype(np.float32)
    return {f"in_{k}": np.ascontiguousarray(v) for k, v in a.items()}, col


def kernel(**inputs):
    import concourse.bacc as bacc
    from concourse.bass_utils import run_bass_kernel_spmd

    arrays, col = layout(inputs)
    nc = bacc.Bacc("TRN2", target_bir_lowering=False, num_devices=1)
    args = {n: nc.dram_tensor(n, a.shape, F32, kind="ExternalInput").ap() for n, a in arrays.items()}
    out = nc.dram_tensor("out", (P, KD, T), F32, kind="ExternalOutput").ap()
    weights = [args[f"in_{name}"][i] for name in ("attn0", "ffn", "attn1", "moe")
               for i in range(arrays[f"in_{name}"].shape[0])]
    vit_tower(nc, args["in_x"], args["in_w_lin"], weights, args["in_small"], args["in_ident"],
              args["in_mask"], out)
    r = run_bass_kernel_spmd(nc, [arrays], core_ids=[0])
    got = r.results[0]["out"]
    return got.transpose(2, 1, 0).reshape(T, D)[col].reshape(B, TOK, D)
```

```python
from contextlib import ExitStack

import concourse.bass as bass
from concourse import mybir

F32 = mybir.dt.float32
F32R = mybir.dt.float32r
BF16 = mybir.dt.bfloat16
I32 = mybir.dt.int32
ALU = mybir.AluOpType
ACT = mybir.ActivationFunctionType
AX_X = mybir.AxisListType.X

P = 128
B, C, IMG, PATCH = 32, 3, 96, 16
SIDE = IMG // PATCH
TOK = SIDE * SIDE + 1
D = 256
KD = D // P
KF = C * PATCH * PATCH // P
HEADS, DH = 16, 64
HD = HEADS * DH
KO = HD // P
FF = 1024
KH = FF // P
E = 8
TOPK = 4 * 256 * 6
NLOG = B * TOK * E

GI = 3
GW = GI * TOK + 1
NG = -(-B // GI)
NTOK = [min(GI, B - g * GI) * TOK for g in range(NG)]
T = (NG - 1) * GW + NTOK[-1]
LAG = 3
GC = 3
CW = GC * GW
NC = -(-NG // GC)
CHUNKS = [(c * CW, min(CW, T - c * CW)) for c in range(NC)]
GROUPS = [list(range(c * GC, min((c + 1) * GC, NG))) for c in range(NC)]
QH = 4
NQ = HEADS // QH
QUADS = [(c, g, t) for c in range(NC) for g in GROUPS[c] for t in range(NQ)]

EPS = 1e-5
UNIT = 256.0
MAGIC = 1.5 * 2.0 ** 23
KNOT = 64.0
MAGIC_KNOT = MAGIC * KNOT
BL = 32
BIG = 3.4028234663852886e38

S_POS = 0
S_CLS = S_POS + KD * TOK
S_BLIN = S_CLS + KD
S_BO = S_BLIN + KD
S_B1F = S_BO + KD
S_B2F = S_B1F + KH
S_B1M = S_B2F + KD
S_B2M = S_B1M + E * KH
S_GATE = S_B2M + KD * E
S_END = S_GATE + KD * E

SPLITS = 4
PIECE = KD * 1024
WSLOTS = 4


def vit_tower(nc, x, w_lin, weights, small, ident_in, mask_in, b1_in, out):
    with ExitStack() as ctx:
        def sb(name, shape, dt=F32):
            return ctx.enter_context(nc.sbuf_tensor(name, shape, dt))

        def sem(name):
            return ctx.enter_context(nc.semaphore(name))

        h = sb("h", [P, KD, T])
        xn = sb("xn", [P, 2, KD, T], F32R)
        wslot = sb("wslot", [P, WSLOTS, 2, PIECE], F32R)
        raw = sb("raw", [P, 2, PIECE])
        hid = sb("hid", [P, 2, 2, KH * CW], F32R)
        work = sb("work", [P, HEADS, CW])
        vbuf = sb("vbuf", [P, 2, HD])
        probs = sb("probs", [P, 4, QH * GW])
        probsT = sb("probsT", [P, 2, QH * GW])
        xc = sb("xc", [P, KD, CW])
        sq = sb("sq", [P, KD, CW])
        rs = sb("rs", [P, CW])
        rt = sb("rt", [P, CW])
        prm = sb("prm", [P, S_END])
        addT = sb("addT", [P, KD, TOK])
        b1r = sb("b1r", [BL + 1, FF], F32R)
        ones_r = sb("ones_r", [BL + 1, CW], F32R)
        b2u = sb("b2u", [P, KD])
        gateR = sb("gateR", [P, 2, KD * E], F32R)
        ident = sb("ident", [P, P])
        identb = sb("identb", [P, P], BF16)
        maskb = sb("maskb", [P, 2, QH, GW], BF16)
        mean_w = sb("mean_w", [P, P])
        c_eps = sb("c_eps", [P, 1])
        c_magic = sb("c_magic", [P, 3])
        c_knot0 = sb("c_knot0", [P, 1])
        c_knot1 = sb("c_knot1", [P, 1])
        negmax = sb("negmax", [P, 4 * QH])
        maxes = sb("maxes", [P, 4 * QH])
        sums = sb("sums", [P, 4 * QH])
        rsum = sb("rsum", [P, 4 * QH])
        count = sb("count", [P, 2])
        sign = sb("sign", [P, 1])
        rank = sb("rank", [P, 1])
        kth = sb("kth", [P, 1])
        found = sb("found", [P, 1], I32)
        tryb = sb("tryb", [P, 1], I32)
        newb = sb("newb", [P, 1], I32)

        logits, keys, below, gates = (probsT[:, 0, i * NG * E:(i + 1) * NG * E] for i in range(4))
        maskf = probsT[:, 1, 0:2 * GW].rearrange("p (l n) -> p l n", l=2)
        b1row = probs[0:BL + 1, :, :].rearrange("p s n -> p (s n)")[:, 0:FF]

        bank = {n: ctx.enter_context(nc.psum_tensor(n, [P, 512], F32))
                for n in ("D0", "D1", "S0", "S1", "T0", "T1", "O0", "O1")}
        BD = [bank["D0"], bank["D1"]]
        BS = [bank["S0"], bank["S1"]]
        BT = [bank["T0"], bank["T1"]]
        BO = [bank["O0"], bank["O1"]]
        BH = BD + BS

        small_in = sem("small_in")
        mats_in = sem("mats_in")
        raw_in = [sem("raw_in0"), sem("raw_in1")]
        patch_in = [sem(f"patch_in{n}") for n in range(NC - 1)]
        high_ready = sem("high_ready")
        start_split = sem("start_split")
        pool_split = sem("pool_split")
        dve_line = sem("dve_line")
        pool_part = sem("pool_part")
        consts = sem("consts")
        params = sem("params")
        masks = sem("masks")
        b1_ready = sem("b1_ready")
        emb_mm = sem("emb_mm")
        h_set = sem("h_set")
        pads = sem("pads")
        ln_mean = [sem(f"ln_mean{n}") for n in range(4)]
        ln_xc = [sem(f"ln_xc{n}") for n in range(4)]
        ln_sq = [sem(f"ln_sq{n}") for n in range(4)]
        ln_var = [sem(f"ln_var{n}") for n in range(4)]
        ln_ln = [sem(f"ln_ln{n}") for n in range(4)]
        ln_rs = [sem(f"ln_rs{n}") for n in range(4)]
        ln_out = [sem(f"ln_out{n}") for n in range(4)]
        qk_mm = [sem(f"qk_mm{n}") for n in range(2)]
        qk_act = [sem(f"qk_act{n}") for n in range(2)]
        v_mm = [sem(f"v_mm{n}") for n in range(2)]
        v_act = [sem(f"v_act{n}") for n in range(2)]
        v_dve = [sem(f"v_dve{n}") for n in range(2)]
        s_mm = [sem(f"s_mm{n}") for n in range(2)]
        s_max = [sem(f"s_max{n}") for n in range(2)]
        s_exp = [sem(f"s_exp{n}") for n in range(2)]
        p_norm = [sem(f"p_norm{n}") for n in range(2)]
        t_mm = [sem(f"t_mm{n}") for n in range(2)]
        t_dve = [sem(f"t_dve{n}") for n in range(2)]
        o_mm = [sem(f"o_mm{n}") for n in range(2)]
        o_high = [sem(f"o_high{n}") for n in range(2)]
        o_low = [sem(f"o_low{n}") for n in range(2)]
        out_mm = [sem(f"out_mm{n}") for n in range(2)]
        h_attn = [sem(f"h_attn{n}") for n in range(2)]
        ff1_mm = sem("ff1_mm")
        ff_t = sem("ff_t")
        ff_abs = sem("ff_abs")
        ff_relu = sem("ff_relu")
        ff_knot = sem("ff_knot")
        ff_y0 = sem("ff_y0")
        ff_y1 = sem("ff_y1")
        ff_dy = sem("ff_dy")
        ff_frac = sem("ff_frac")
        ff_lin = sem("ff_lin")
        y0_gated = sem("y0_gated")
        ff_q = sem("ff_q")
        ff_sum = sem("ff_sum")
        ff_hid = sem("ff_hid")
        ff2_mm = sem("ff2_mm")
        ff2_ev = sem("ff2_ev")
        h_ff = sem("h_ff")
        log_mm = sem("log_mm")
        cnt_ready = sem("cnt_ready")
        cnt_mm = sem("cnt_mm")
        gates_ready = sem("gates_ready")
        gb_mm = sem("gb_mm")
        gb_act = sem("gb_act")
        m1_mm = sem("m1_mm")
        m_gelu = sem("m_gelu")
        m_high = sem("m_high")
        m_hid = sem("m_hid")
        m2_mm = sem("m2_mm")
        m_y = sem("m_y")
        h_moe = sem("h_moe")
        stored = sem("stored")

        FIRST_W = 1 + NC
        NSTART = FIRST_W + 2
        NPIECE = FIRST_W + len(weights)

        def piece_split(i):
            return (start_split, i + 1) if i < NSTART else (pool_split, i - NSTART + 1)

        def piece_place(i):
            if i == 0:
                return [wslot[:, WSLOTS - 1, k, 0:KF * D] for k in range(2)]
            if i < FIRST_W:
                c = i - 1
                return [hid[:, c % 2, k, 0:KF * CHUNKS[c][1]] for k in range(2)]
            return [wslot[:, (i - FIRST_W) % WSLOTS, k, :] for k in range(2)]

        def piece_raw(i):
            if 2 <= i <= 3:
                n = KF * CW
                return work[:, :, :].rearrange("p m n -> p (m n)")[:, (i - 2) * n:(i - 2) * n + piece_size(i)]
            if i == 4:
                return vbuf[:, :, :].rearrange("p s n -> p (s n)")[:, 0:piece_size(i)]
            return raw[:, (i if i < 2 else i - 3) % 2, 0:piece_size(i)]

        def landed(eng, i):
            if 2 <= i <= 4:
                eng.wait_ge(patch_in[i - 2], 16)
            else:
                k = i if i < 2 else i - 3
                eng.wait_ge(raw_in[k % 2], 16 * (k // 2 + 1))

        def piece_size(i):
            return KF * D if i == 0 else KF * CHUNKS[i - 1][1] if i < FIRST_W else PIECE

        def place_free(i):
            if i < FIRST_W:
                return (emb_mm, KD * (i - 2)) if i >= 3 else None
            j = i - FIRST_W
            if j < WSLOTS - 1:
                return None
            return [(emb_mm, KD * NC),
                    (qk_mm[0], 16 * (NC - 1) + 8), (qk_mm[0], 16 * NC), (v_mm[0], 2 * NG), (out_mm[0], KD * NC),
                    (ff1_mm, KH * NC), (ff2_mm, KD * NC),
                    (qk_mm[1], 16 * (NC - 1) + 8), (qk_mm[1], 16 * NC), (v_mm[1], 2 * NG), (out_mm[1], KD * NC),
                    ][j - 3] if j < 14 else ((m1_mm, m2_mm)[j % 2], (KH, KD)[j % 2] * NC * ((j - 14) // 2 + 1))

        W_QKVO = [0, 6]
        W_FF, W_MOE = 4, 10

        def weight(j, k, width):
            return wslot[:, j % WSLOTS, k, :].rearrange("p (a n) -> p a n", n=width)

        def wait_weight(eng, j):
            eng.wait_ge(*piece_split(FIRST_W + j))

        def heads(t):
            return [2 * QH * (t // 2) + t % 2 + 2 * i for i in range(QH)]

        def cols(g):
            return slice(g * GW, g * GW + NTOK[g])

        def ff_bufs(s):
            w = CHUNKS[s // KH][1]
            return [work[:, 5 * (s % 3) + k, 0:w] for k in range(5)]

        def ff_pool_diff(pool, s):
            v, a, kn, y0, y1 = ff_bufs(s)
            pool.wait_ge(ff_y1, s + 1)
            nc.gpsimd.tensor_tensor(y1, y1, y0, ALU.subtract).then_inc(ff_dy, 1)

        def ff_pool_sum(pool, s):
            v, a, kn, y0, y1 = ff_bufs(s)
            pool.wait_ge(ff_q, s + 1)
            nc.gpsimd.tensor_tensor(y0, y0, v, ALU.add).then_inc(ff_sum, 1)

        def moe_add(pool, e, c, dc):
            a, w = CHUNKS[c]
            j = (e * NC + c) * KD + dc
            pool.wait_ge(m_y, j + 1)
            if j >= KD * NC:
                pool.wait_ge(h_moe, j - KD * NC + 1)
            nc.gpsimd.tensor_tensor(h[:, dc, a:a + w], h[:, dc, a:a + w], moe_y(j)[:, 0:w],
                                    ALU.add).then_inc(h_moe, 1)

        def moe_first(pool, j):
            c, dc = j // KD, j % KD
            a, w = CHUNKS[c]
            pool.wait_ge(gb_act, c + 1)
            pool.wait_ge(m_y, j + 1)
            y = moe_y0(j)[:, 0:w]
            nc.gpsimd.tensor_tensor(y, y, moe_gate(0, c)[:, 0:w], ALU.mult).then_inc(y0_gated, 1)
            pool.wait_ge(y0_gated, j + 1)
            nc.gpsimd.tensor_tensor(h[:, dc, a:a + w], h[:, dc, a:a + w], y, ALU.add).then_inc(h_moe, 1)

        def moe_y0(j):
            return vbuf[:, j // 3, j % 3 * CW:(j % 3 + 1) * CW] if j < 6 else probs[:, j - 6, 0:CW]

        def moe_g(s):
            return work[:, s % 4, :]

        def moe_y(j):
            return work[:, 4 + j % 4, :]

        def moe_gate(e, c):
            return work[:, 8 + (e % 2) * NC + c, :]

        def heads_out(k, c, t, a, nt):
            m = QH * (t // 2)
            return hid[:, c % 2, k, :].rearrange("p (m n) -> p m n", n=CW)[:, m:m + QH, a:a + nt]

        def out_pair(pair, nt):
            return BO[pair % 2][:, 0:QH * GW].rearrange("p (m n) -> p m n", n=GW)[:, :, 0:nt]

        def quads(c):
            mine = [q for q in range(len(QUADS)) if QUADS[q][0] == c]
            return mine, range(mine[0], mine[-1] + LAG + 2)

        def qk_sides(l, c):
            return [(2 * l, i) for i in range(2 - l, NC)] if c == 0 else [(2 * l + 1, c - 1)]

        block = ctx.enter_context(nc.Block())

        @block.sync
        def _(sp):
            for i in range(NPIECE):
                if i == FIRST_W or i == FIRST_W + 1:
                    sp.wait_ge(*piece_split(i - FIRST_W))
                elif i > FIRST_W + 1:
                    sp.wait_ge(*piece_split(i - 2))
                if i == 0:
                    src = w_lin
                elif i < FIRST_W:
                    a, w = CHUNKS[i - 1]
                    src = x[:, :, a:a + w]
                else:
                    src = weights[i - FIRST_W]
                dst = piece_raw(i)
                if 0 < i < FIRST_W:
                    dst = dst.rearrange("p (k n) -> p k n", k=KF)
                sp.dma_start(dst, src).then_inc(patch_in[i - 2] if 2 <= i <= 4 else raw_in[(i if i < 2 else i - 3) % 2], 16)
                if i == 1:
                    sp.dma_start(prm[:, :], small).then_inc(small_in, 16)
                    sp.dma_start(ident[:, :], ident_in).then_inc(mats_in, 16)
                    sp.dma_start(maskf, mask_in).then_inc(mats_in, 16)
                    sp.dma_start(b1row[0:1, :], b1_in).then_inc(mats_in, 16)
                    sp.dma_start(b1row[BL:BL + 1, :], b1_in).then_inc(mats_in, 16)
            for c, (a, w) in enumerate(CHUNKS):
                sp.wait_ge(h_moe, KD * NC * (E - 1) + KD * (c + 1))
                sp.dma_start(out[:, :, a:a + w], h[:, :, a:a + w]).then_inc(stored, 16)
            sp.wait_ge(stored, 16 * NC)

        @block.gpsimd
        def _(pool):
            nc.gpsimd.memset(mean_w[:, :], 1.0 / D).then_inc(consts, 1)
            nc.gpsimd.memset(c_eps[:, :], EPS).then_inc(consts, 1)
            nc.gpsimd.memset(ones_r[:, :].bitcast(F32), 1.0).then_inc(consts, 1)
            nc.gpsimd.memset(b1r[:, :].bitcast(F32), 0.0).then_inc(consts, 1)
            for k, value in enumerate((MAGIC, -MAGIC, -MAGIC / 4)):
                nc.gpsimd.memset(c_magic[:, k:k + 1], value).then_inc(consts, 1)
            nc.gpsimd.memset(c_knot0[:, :], MAGIC_KNOT / UNIT).then_inc(consts, 1)
            nc.gpsimd.memset(c_knot1[:, :], (MAGIC_KNOT - KNOT) / UNIT).then_inc(consts, 1)

            def split(i):
                pool.wait_ge(high_ready, i + 1)
                high, low = piece_place(i)
                nc.gpsimd.tensor_tensor(low, piece_raw(i), high.bitcast(F32), ALU.subtract).then_inc(pool_split, 1)

            def split_part(i, k):
                pool.wait_ge(high_ready, i + 1)
                high, low = piece_place(i)
                sl = slice(k * PIECE // SPLITS, (k + 1) * PIECE // SPLITS)
                nc.gpsimd.tensor_tensor(low[:, sl], piece_raw(i)[:, sl], high.bitcast(F32)[:, sl],
                                        ALU.subtract).then_inc(pool_split if k == SPLITS - 1 else pool_part, 1)

            for i in range(NSTART, FIRST_W + W_FF + 2):
                split(i)
            for s in range(KH * NC + 1):
                if KH + 3 <= s < 3 * KH + 3 and s % KH in (3, 5, 7, 1):
                    k = (s - KH - 3) // 2
                    split_part(FIRST_W + W_FF + 2 + k // SPLITS, k % SPLITS)
                if s >= 1:
                    ff_pool_sum(pool, s - 1)
                if s < KH * NC:
                    ff_pool_diff(pool, s)
            for i in range(FIRST_W + 8, FIRST_W + W_MOE + 4):
                split(i)
            for e in range(1, E):
                for c in range(NC):
                    if c == 0 and e + 1 < E:
                        for i in (2, 3):
                            split(FIRST_W + W_MOE + 2 * e + i)
                    if e == 1 and c == 0:
                        for j in range(KD * NC):
                            moe_first(pool, j)
                    for dc in range(KD):
                        moe_add(pool, e, c, dc)

        def split_products(pe, psum, w, xs, n, last_sem, between=None, first=True):
            k = 0
            for i in range(n):
                (wh, wl), (xh, xl) = w(i), xs(i)
                for a, b in ((wh, xh), (wh, xl), (wl, xh)):
                    mm = pe.matmul(psum, a, b, start=(first and k == 0), stop=(k == 3 * n - 1))
                    k += 1
                if between is not None and i == n // 2 - 1:
                    between()
            mm.then_inc(last_sem, 1)

        @block.tensor
        def _(pe):
            def hidden(slot, kk, a, w):
                return [hid[:, slot, k, kk * CW + a:kk * CW + a + w] for k in range(2)]

            def normed(kk, sl):
                return [xn[:, k, kk, sl] for k in range(2)]

            def embed(c):
                a, w = CHUNKS[c]
                pe.wait_ge(*piece_split(1 + c))
                for dc in range(KD):
                    if c >= 1:
                        pe.wait_ge(h_set, KD * (c - 1) + dc + 1)
                    wl = [wslot[:, WSLOTS - 1, k, 0:KF * D].rearrange("p (a n) -> p a n", n=D) for k in range(2)]
                    split_products(pe, BD[dc][:, 0:w],
                                   lambda i: [t[:, i, dc * P:(dc + 1) * P] for t in wl],
                                   lambda i: [hid[:, c % 2, k, i * w:(i + 1) * w] for k in range(2)],
                                   KF, emb_mm)

            NORMED = [h_set, h_attn[0], h_ff, h_attn[1]]

            def mean(n, c):
                a, w = CHUNKS[c]
                pe.wait_ge(NORMED[n], KD * (c + 1))
                if c >= 1:
                    pe.wait_ge(ln_xc[n], c)
                for k in range(KD):
                    mm = pe.matmul(BT[0][:, 0:w], mean_w[:, :], h[:, k, a:a + w],
                                   start=(k == 0), stop=(k == KD - 1))
                mm.then_inc(ln_mean[n], 1)

            def variance(n, c):
                a, w = CHUNKS[c]
                pe.wait_ge(ln_sq[n], c + 1)
                if c >= 1:
                    pe.wait_ge(ln_out[n], c)
                for k in range(KD):
                    mm = pe.matmul(BT[1][:, 0:w], mean_w[:, :], sq[:, k, 0:w],
                                   start=(k == 0), stop=(k == KD - 1))
                mm.then_inc(ln_var[n], 1)

            def attention(l, n):
                q_w, k_w, v_w, o_w = (W_QKVO[l] + i for i in range(4))

                def project_qk(c):
                    a, w = CHUNKS[c]
                    pe.wait_ge(ln_out[n], c + 1)
                    for m in range(2 * KO):
                        j = 2 * KO * c + m
                        wj = (q_w, k_w)[m // KO]
                        if c == 0 and m % KO == 0:
                            wait_weight(pe, wj)
                        if m >= 4:
                            pe.wait_ge(qk_act[l], j - 3)
                        elif m < 2 and c >= 1:
                            pe.wait_ge(h_attn[l], KD * (c - 1) + m + 1)
                        elif m < 2 and l == 0:
                            pe.wait_ge(h_set, KD * (NC - 1) + m + 1)
                        elif l == 1 and c == 0:
                            pe.wait_ge(ff_t, KH * NC - 3 + m)
                        mc = m % KO
                        split_products(pe, BH[m % 4][:, 0:w],
                                       lambda i: [weight(wj, k, HD)[:, i, mc * P:(mc + 1) * P] for k in range(2)],
                                       lambda i: normed(i, slice(a, a + w)), KD, qk_mm[l])
                        for k, side in enumerate(qk_sides(l, c)):
                            if m == 5 * k:
                                mean(*side)
                            if m == 5 * k + 4:
                                variance(*side)

                def project_v(g):
                    if g == 0:
                        wait_weight(pe, v_w)
                    c = g // GC
                    for half in range(2):
                        if g % GC == 0 and g > 0:
                            pe.wait_ge((v_act, v_dve)[half][l], g)
                        elif g % GC == 0:
                            pe.wait_ge(qk_act[l], 2 * KO - 3 + half)
                        elif g % GC == 1 and g > 1:
                            pe.wait_ge(qk_act[l], 2 * KO * (c + 1) - 3 + half)
                        else:
                            pe.wait_ge((v_act, v_dve)[half][l], g)
                        split_products(pe, BD[half][0:NTOK[g], :],
                                       lambda i: normed(i, cols(g)),
                                       lambda i: [weight(v_w, k, HD)[:, i, half * 512:(half + 1) * 512]
                                                  for k in range(2)], KD, v_mm[l])

                def scores(q):
                    c, g, t = QUADS[q]
                    nt, a = NTOK[g], g * GW - CHUNKS[c][0]
                    if q == 0:
                        pe.wait_ge(masks, 2)
                        pe.wait_ge(mats_in, 64)
                    if t == 0 and g % GC == 0:
                        pe.wait_ge(qk_act[l], 2 * KO * (c + 1))
                    if q >= 2:
                        pe.wait_ge(s_exp[l], QH * (q - 1))
                    bank4 = BS[q % 2][0:nt, 0:QH * GW].rearrange("p (h n) -> p h n", h=QH)[:, :, 0:nt]
                    pe.matmul(bank4, identb[0:nt, 0:nt], maskb[0:nt, l, :, 0:nt], start=True, stop=False,
                              skip_group_check=True)
                    r = DH * (t % 2)
                    for i, hd in enumerate(heads(t)):
                        mm = pe.matmul(BS[q % 2][0:nt, i * GW:i * GW + nt],
                                       work[r:r + DH, hd // 2, a:a + nt], work[r:r + DH, KO + hd // 2, a:a + nt],
                                       start=False, stop=(i == QH - 1), skip_group_check=True)
                    mm.then_inc(s_mm[l], 1)

                def transposes(q):
                    c, g, t = QUADS[q]
                    nt = NTOK[g]
                    pe.wait_ge(p_norm[l], q + 1)
                    if t == 0 and g % GC == 0:
                        pe.wait_ge(ln_out[qk_sides(l, c)[-1][0]], qk_sides(l, c)[-1][1] + 1)
                    if q >= 2:
                        pe.wait_ge(t_dve[l], q - 1)
                    for i in range(QH):
                        mm = pe.transpose(BT[q % 2][0:nt, i * GW:i * GW + nt],
                                          probs[0:nt, q % 4, i * GW:i * GW + nt], ident[0:nt, 0:nt])
                    mm.then_inc(t_mm[l], 1)

                def values(q):
                    c, g, t = QUADS[q]
                    nt = NTOK[g]
                    pe.wait_ge(t_dve[l], q + 1)
                    if t == 0:
                        pe.wait_ge(v_act[l], g + 1)
                        pe.wait_ge(v_dve[l], g + 1)
                    if q >= 4:
                        pe.wait_ge(o_low[l], q // 2 - 1)
                    r = DH * (t % 2)
                    for i, hd in enumerate(heads(t)):
                        mm = pe.matmul(BO[q // 2 % 2][r:r + DH, i * GW:i * GW + nt],
                                       vbuf[0:nt, g % 2, hd * DH:(hd + 1) * DH],
                                       probsT[0:nt, q % 2, i * GW:i * GW + nt], start=True, stop=True,
                                       skip_group_check=True)
                    mm.then_inc(o_mm[l], 1)

                def project_out(c):
                    a, w = CHUNKS[c]
                    if c == 0:
                        wait_weight(pe, o_w)
                    pe.wait_ge(o_low[l], NQ // 2 * (GROUPS[c][-1] + 1))
                    for dc in range(KD):
                        pe.wait_ge((v_act, v_dve)[dc][l], min(GROUPS[c][-1] + 2, NG))
                        split_products(pe, BD[dc][:, 0:w],
                                       lambda i: [weight(o_w, k, D)[:, i, dc * P:(dc + 1) * P] for k in range(2)],
                                       lambda i: hidden(c % 2, i, 0, w), KO, out_mm[l])

                for c in range(NC):
                    project_qk(c)
                    mine, steps = quads(c)
                    if c == 0:
                        project_v(0)
                    for q in steps:
                        if q in mine:
                            scores(q)
                        if q in mine and q % NQ == 3 and q // NQ + 1 < NG:
                            project_v(q // NQ + 1)
                        if q - LAG in mine:
                            transposes(q - LAG)
                        if q - LAG - 1 in mine:
                            values(q - LAG - 1)
                    project_out(c)

            pe.wait_ge(*piece_split(0))
            embed(0)
            embed(1)
            pe.wait_ge(consts, 1)
            mean(0, 0)
            embed(2)
            variance(0, 0)
            mean(0, 1)
            embed(3)
            variance(0, 1)
            attention(0, 0)

            def ff_up(c):
                a, w = CHUNKS[c]
                pe.wait_ge(ln_out[1], c + 1)
                if c == 0:
                    wait_weight(pe, W_FF)
                for m in range(KH):
                    s = KH * c + m
                    if s >= 4:
                        pe.wait_ge(ff_t, s - 3)
                    elif s < 2:
                        pe.wait_ge(h_attn[0], KD * (NC - 1) + s + 1)
                    if s == 0:
                        pe.wait_ge(b1_ready, 3)
                    pe.matmul(BH[s % 4][:, 0:w], b1r[:, m * P:(m + 1) * P], ones_r[:, 0:w], start=True, stop=False)
                    split_products(pe, BH[s % 4][:, 0:w],
                                   lambda i: [weight(W_FF, k, FF)[:, i, m * P:(m + 1) * P] for k in range(2)],
                                   lambda i: normed(i, slice(a, a + w)), KD, ff1_mm, first=False)
                    if c == 0 and m == 0:
                        mean(1, 3)
                    if c == 0 and m == 4:
                        variance(1, 3)

            def ff_down(c):
                a, w = CHUNKS[c]
                pe.wait_ge(ff_hid, KH * (c + 1))
                if c == 0:
                    wait_weight(pe, W_FF + 1)
                for dc in range(KD):
                    if c >= 1:
                        pe.wait_ge(ff2_ev, KD * (c - 1) + dc + 1)
                    split_products(pe, BO[dc][:, 0:w],
                                   lambda i: [weight(W_FF + 1, k, D)[:, i, dc * P:(dc + 1) * P] for k in range(2)],
                                   lambda i: hidden(c % 2, i, 0, w), KH, ff2_mm)
                    if c == 1 and dc == 1:
                        mean(2, 0)
                    if c == 2 and dc == 0:
                        variance(2, 0)

            for c in range(NC):
                ff_up(c)
                if c >= 1:
                    ff_down(c - 1)
            ff_down(NC - 1)
            attention(1, 2)
            mean(3, 3)

            def router():
                pe.wait_ge(params, 5)
                for g in range(NG):
                    pe.wait_ge(ln_out[3], g // GC + 1)
                    split_products(pe, BO[0][0:NTOK[g], g * E:(g + 1) * E],
                                   lambda i: normed(i, cols(g)),
                                   lambda i: [gateR[:, k, i * E:(i + 1) * E] for k in range(2)], KD,
                                   log_mm)

            def sum_counts(i):
                pe.wait_ge(cnt_ready, i + 1)
                pe.matmul(BT[1][:, 0:1], mean_w[:, :], count[:, i % 2:i % 2 + 1], start=True,
                          stop=True).then_inc(cnt_mm, 1)

            def moe_up(e, c):
                a, w = CHUNKS[c]
                if c == 0:
                    wait_weight(pe, W_MOE + 2 * e)
                for m in range(KH):
                    s = (e * NC + c) * KH + m
                    if s >= 4:
                        pe.wait_ge(m_gelu, s - 3)
                    split_products(pe, BH[s % 4][:, 0:w],
                                   lambda i: [weight(W_MOE + 2 * e, k, FF)[:, i, m * P:(m + 1) * P] for k in range(2)],
                                   lambda i: normed(i, slice(a, a + w)), KD, m1_mm)
                    if s == 4:
                        variance(3, 3)
                    n = e * NC + c
                    if m % 2 and 1 <= n <= 5:
                        i = 8 * (n - 1) + m // 2 - 1
                        if 0 <= i < 32:
                            sum_counts(i)

            def spread_gates(e):
                for c, (a, w) in enumerate(CHUNKS):
                    j = e * NC + c
                    if j >= 2:
                        pe.wait_ge(gb_act, j - 1)
                    for g in GROUPS[c]:
                        wd = min(GW, w - (g * GW - a))
                        nt = NTOK[g]
                        mm = pe.matmul(BT[j % 2][:, g * GW - a:g * GW - a + wd],
                                       gates[0:nt, g * E + e:g * E + e + 1].to_broadcast([nt, P]),
                                       ident[0:nt, 0:wd], start=True, stop=True)
                    mm.then_inc(gb_mm, 1)

            def moe_down(e, c):
                a, w = CHUNKS[c]
                j = e * NC + c
                pe.wait_ge(m_hid, KH * (j + 1))
                if c == 0:
                    wait_weight(pe, W_MOE + 2 * e + 1)
                for dc in range(KD):
                    if j >= 1:
                        pe.wait_ge(m_y, KD * (j - 1) + dc + 1)
                    split_products(pe, BO[dc][:, 0:w],
                                   lambda i: [weight(W_MOE + 2 * e + 1, k, D)[:, i, dc * P:(dc + 1) * P]
                                              for k in range(2)],
                                   lambda i: hidden(j % 2, i, 0, w), KH, m2_mm,
                                   between=(lambda: sum_counts(8 * j + 3 + 2 * dc)) if e == 0 else None)
                    if e == 0:
                        sum_counts(8 * j + 4 + 2 * dc)

            steps = [(e, c) for e in range(E) for c in range(NC)]
            for n, (e, c) in enumerate(steps):
                moe_up(e, c)
                if n == 0:
                    router()
                if n == NC + 1:
                    pe.wait_ge(gates_ready, 1)
                    spread_gates(0)
                if c == 1 and e >= 1:
                    spread_gates(e)
                if n >= 1:
                    moe_down(*steps[n - 1])
            moe_down(*steps[-1])

        @block.scalar
        def _(act):
            def high_part(i):
                landed(act, i)
                if place_free(i):
                    act.wait_ge(*place_free(i))
                nc.scalar.activation(piece_place(i)[0], piece_raw(i), ACT.Copy).then_inc(high_ready, 1)

            for i in range(FIRST_W):
                high_part(i)
            act.wait_ge(consts, 9)
            act.wait_ge(small_in, 16)

            def square(n, c):
                w = CHUNKS[c][1]
                act.wait_ge(ln_xc[n], c + 1)
                if c >= 1:
                    act.wait_ge(ln_var[n], c)
                nc.scalar.activation(sq[:, :, 0:w], xc[:, :, 0:w], ACT.Square).then_inc(ln_sq[n], 1)

            def inv_root(n, c):
                w = CHUNKS[c][1]
                act.wait_ge(ln_var[n], c + 1)
                if c >= 1:
                    act.wait_ge(ln_out[n], c)
                nc.scalar.activation(rt[:, 0:w], BT[1][:, 0:w], ACT.Ln,
                                     bias=c_eps[:, 0:1]).then_inc(ln_ln[n], 1)
                act.wait_ge(ln_ln[n], c + 1)
                nc.scalar.activation(rs[:, 0:w], rt[:, 0:w], ACT.Exp, scale=-0.5).then_inc(ln_rs[n], 1)

            def attention(l):
                def move_q(c):
                    w = CHUNKS[c][1]
                    for m in range(2 * KO):
                        act.wait_ge(qk_mm[l], 2 * KO * c + m + 1)
                        nc.scalar.activation(work[:, m, 0:w], BH[m % 4][:, 0:w], ACT.Copy).then_inc(qk_act[l], 1)
                        for k, side in enumerate(qk_sides(l, c)):
                            if m == 5 * k + 1:
                                square(*side)
                            if m == 5 * k + 4:
                                inv_root(*side)

                def move_v(g):
                    act.wait_ge(v_mm[l], 2 * g + 1)
                    if g >= 2:
                        act.wait_ge(o_mm[l], NQ * (g - 1))
                    nc.scalar.activation(vbuf[0:NTOK[g], g % 2, 0:512], BD[0][0:NTOK[g], :],
                                         ACT.Copy).then_inc(v_act[l], 1)

                def exps(q):
                    c, g, t = QUADS[q]
                    nt = NTOK[g]
                    act.wait_ge(s_max[l], q + 1)
                    if q >= 4:
                        act.wait_ge(t_mm[l], q - 3)
                    for i in range(QH):
                        k = QH * (q % 4) + i
                        nc.scalar.activation(probs[0:nt, q % 4, i * GW:i * GW + nt],
                                             BS[q % 2][0:nt, i * GW:i * GW + nt], ACT.Exp,
                                             bias=negmax[0:nt, k:k + 1], scale=DH ** -0.5,
                                             accum_out=sums[0:nt, k:k + 1]).then_inc(s_exp[l], 1)

                def high_out(pair):
                    c, g, t = QUADS[2 * pair]
                    nt, a = NTOK[g], g * GW - CHUNKS[c][0]
                    act.wait_ge(o_mm[l], 2 * pair + 2)
                    if c >= 2:
                        act.wait_ge(out_mm[l], KD * (c - 1))
                    nc.scalar.activation(heads_out(0, c, t, a, nt), out_pair(pair, nt),
                                         ACT.Copy).then_inc(o_high[l], 1)

                for c in range(NC):
                    move_q(c)
                    if c == NC - 1:
                        high_part(FIRST_W + W_QKVO[l] + 4)
                        high_part(FIRST_W + W_QKVO[l] + 5)
                    mine, steps = quads(c)
                    if c == 0:
                        move_v(0)
                    for q in steps:
                        if q in mine:
                            exps(q)
                        if q in mine and q % NQ == 3 and q // NQ + 1 < NG:
                            move_v(q // NQ + 1)
                        if q - LAG - 1 in mine and (q - LAG - 1) % 2:
                            high_out((q - LAG - 1) // 2)

            square(0, 0)
            inv_root(0, 0)
            high_part(FIRST_W)
            square(0, 1)
            high_part(FIRST_W + 1)
            inv_root(0, 1)
            high_part(FIRST_W + 2)
            high_part(FIRST_W + 3)
            attention(0)

            def ff_load(s):
                v, a, kn, y0, y1 = ff_bufs(s)
                act.wait_ge(ff1_mm, s + 1)
                if s >= 3:
                    act.wait_ge(ff_sum, s - 2)
                nc.scalar.activation(v, BH[s % 4][:, 0:CHUNKS[s // KH][1]], ACT.Identity,
                                     bias=c_magic[:, 0:1], scale=UNIT).then_inc(ff_t, 1)

            def ff_shape(s):
                v, a, kn, y0, y1 = ff_bufs(s)
                act.wait_ge(ff_t, s + 1)
                if s >= 3:
                    act.wait_ge(ff_q, s - 2)
                nc.scalar.activation(a, v, ACT.Abs, bias=c_magic[:, 1:2]).then_inc(ff_abs, 1)
                act.wait_ge(ff_abs, s + 1)
                nc.scalar.activation(v, v, ACT.Relu, bias=c_magic[:, 2:3], scale=0.25).then_inc(ff_relu, 1)

            def ff_knots(s):
                v, a, kn, y0, y1 = ff_bufs(s)
                act.wait_ge(ff_knot, s + 1)
                nc.scalar.activation(y0, kn, ACT.Gelu, bias=c_knot0[:, 0:1], scale=-1.0 / UNIT).then_inc(ff_y0, 1)
                nc.scalar.activation(y1, kn, ACT.Gelu, bias=c_knot1[:, 0:1], scale=-1.0 / UNIT).then_inc(ff_y1, 1)

            NS = KH * NC
            square(1, 3)
            ff_load(0)
            ff_shape(0)
            for s in range(NS):
                if s + 1 < NS:
                    ff_load(s + 1)
                    ff_shape(s + 1)
                ff_knots(s)
                if s == 3:
                    inv_root(1, 3)
                if s % KH == 1 and s // KH in (1, 2):
                    high_part(FIRST_W + W_FF + 1 + s // KH)
                if s == 2 * KH + 6:
                    square(2, 0)
            inv_root(2, 0)
            for i in (8, 9):
                high_part(FIRST_W + i)
            attention(1)
            square(3, 3)

            def spread(e):
                for c, (a, w) in enumerate(CHUNKS):
                    j = e * NC + c
                    act.wait_ge(gb_mm, j + 1)
                    if e >= 2:
                        act.wait_ge(m_y, KD * ((e - 2) * NC + c + 1))
                    nc.scalar.activation(moe_gate(e, c)[:, 0:w], BT[j % 2][:, 0:w], ACT.Copy).then_inc(gb_act, 1)

            for s in range(E * NC * KH):
                e, c, m = s // (NC * KH), s // KH % NC, s % KH
                w = CHUNKS[c][1]
                act.wait_ge(m1_mm, s + 1)
                if s == 6:
                    inv_root(3, 3)
                if s in (10, 12):
                    high_part(FIRST_W + W_MOE + s // 2 - 3)
                if e >= 1 and e + 1 < E and (c, m) in ((0, 1), (1, 4)):
                    high_part(FIRST_W + W_MOE + 2 * e + 2 + c)
                if s >= 4:
                    act.wait_ge(m_hid, s - 3)
                nc.scalar.activation(moe_g(s)[:, 0:w], BH[s % 4][:, 0:w], ACT.Gelu_apprx_tanh,
                                     bias=prm[:, S_B1M + e * KH + m:S_B1M + e * KH + m + 1]).then_inc(m_gelu, 1)
                if c == 1 and m == KH - 1 and e >= 1:
                    if e == 1:
                        spread(0)
                    spread(e)

        @block.vector
        def _(dve):
            done = [0]

            def tick(ins):
                done[0] += 1
                ins.then_inc(dve_line, 1)
                return done[0]

            def link(ins):
                dve.wait_ge(dve_line, tick(ins))

            dve.wait_ge(small_in, 16)
            pos = prm[:, S_POS:S_CLS].rearrange("p (k n) -> p k n", k=KD)
            for k in range(KD):
                nc.vector.tensor_scalar(addT[:, k, 1:TOK], pos[:, k, 1:TOK], prm[:, S_BLIN + k:S_BLIN + k + 1],
                                        None, ALU.add).then_inc(params, 1)
            nc.vector.tensor_tensor(addT[:, :, 0], pos[:, :, 0], prm[:, S_CLS:S_BLIN], ALU.add).then_inc(params, 1)
            tick(nc.vector.tensor_scalar(b2u[:, :], prm[:, S_B2F:S_B1M], UNIT, None, ALU.mult))
            nc.vector.tensor_copy(gateR[:, 0, :], prm[:, S_GATE:S_END]).then_inc(params, 1)
            dve.wait_ge(params, 4)
            nc.vector.tensor_tensor(gateR[:, 1, :], prm[:, S_GATE:S_END], gateR[:, 0, :].bitcast(F32),
                                    ALU.subtract).then_inc(params, 1)
            nc.vector.memset(h[:, :, 0:(NG - 1) * GW].rearrange("p k (g n) -> p k g n", n=GW)[:, :, :, GW - 1:GW],
                             0.0).then_inc(pads, 1)

            def low_part(i):
                dve.wait_ge(high_ready, i + 1)
                high, low = piece_place(i)
                nc.vector.tensor_tensor(low, piece_raw(i), high.bitcast(F32), ALU.subtract).then_inc(start_split, 1)

            def set_h(c):
                for dc in range(KD):
                    dve.wait_ge(emb_mm, KD * c + dc + 1)
                    for g in GROUPS[c]:
                        ni = NTOK[g] // TOK
                        a = g * GW - CHUNKS[c][0]
                        ins = nc.vector.tensor_tensor(
                            h[:, dc, cols(g)].rearrange("p (i n) -> p i n", n=TOK),
                            BD[dc][:, a:a + NTOK[g]].rearrange("p (i n) -> p i n", n=TOK),
                            addT[:, dc:dc + 1, :].to_broadcast([P, ni, TOK]), ALU.add)
                    ins.then_inc(h_set, 1)

            def center(n, c):
                a, w = CHUNKS[c]
                dve.wait_ge(ln_mean[n], c + 1)
                if c >= 1:
                    dve.wait_ge(ln_out[n], c)
                elif n >= 1:
                    dve.wait_ge(ln_out[n - 1], NC)
                mean = BT[0][:, 0:w].rearrange("p (a n) -> p a n", a=1).to_broadcast([P, KD, w])
                nc.vector.tensor_tensor(xc[:, :, 0:w], h[:, :, a:a + w], mean,
                                        ALU.subtract).then_inc(ln_xc[n], 1)

            def finish(n, c):
                a, w = CHUNKS[c]
                dve.wait_ge(ln_rs[n], c + 1)
                r, t = rs[:, 0:w], rt[:, 0:w]
                link(nc.vector.tensor_tensor(t, r, r, ALU.mult))
                link(nc.vector.scalar_tensor_tensor(t, BT[1][:, 0:w], EPS, t, ALU.add, ALU.mult))
                link(nc.vector.tensor_scalar(t, t, -0.5, 1.5, ALU.mult, ALU.add))
                link(nc.vector.tensor_tensor(r, t, r, ALU.mult))
                x2 = xc[:, :, 0:w]
                rb = rs[:, 0:w].rearrange("p (a n) -> p a n", a=1).to_broadcast([P, KD, w])
                link(nc.vector.tensor_tensor(x2, x2, rb, ALU.mult))
                link(nc.vector.tensor_copy(xn[:, 0, :, a:a + w], x2))
                nc.vector.tensor_tensor(xn[:, 1, :, a:a + w], x2, xn[:, 0, :, a:a + w].bitcast(F32),
                                        ALU.subtract).then_inc(ln_out[n], 1)

            low_part(0)
            low_part(1)
            dve.wait_ge(params, 3)
            for c in range(NC):
                low_part(c + 2)
                set_h(c)
                if c >= 2:
                    finish(0, c - 2)
                if c >= 1 and c <= 2:
                    center(0, c - 1)
            low_part(FIRST_W + 1)
            dve.wait_ge(mats_in, 64)
            dve.wait_ge(consts, 9)
            for row in (0, BL):
                nc.vector.tensor_copy(b1r[row:row + 1, :], b1row[row:row + 1, :]).then_inc(b1_ready, 1)
            dve.wait_ge(b1_ready, 2)
            low = b1r[BL:BL + 1, :]
            nc.vector.tensor_tensor(low, b1row[BL:BL + 1, :], low.bitcast(F32), ALU.subtract).then_inc(b1_ready, 1)
            nc.vector.tensor_copy(identb[:, :], ident[:, :]).then_inc(masks, 1)
            for l in range(2):
                for i in range(QH):
                    ins = nc.vector.tensor_copy(maskb[:, l, i, :], maskf[:, l, :])
            ins.then_inc(masks, 1)
            dve.wait_ge(emb_mm, KD * NC)
            nc.vector.memset(hid[:, :, :, :].rearrange("p s k (m n) -> p (s k m) n", n=GW)[:, :, GW - 1:GW].bitcast(F32),
                             0.0).then_inc(pads, 1)

            def attention(l):
                def move_v(g):
                    dve.wait_ge(v_mm[l], 2 * g + 2)
                    if g >= 2:
                        dve.wait_ge(o_mm[l], NQ * (g - 1))
                    nc.vector.tensor_copy(vbuf[0:NTOK[g], g % 2, 512:HD], BD[1][0:NTOK[g], :]).then_inc(v_dve[l], 1)

                def row_max(q):
                    c, g, t = QUADS[q]
                    nt = NTOK[g]
                    dve.wait_ge(s_mm[l], q + 1)
                    k = QH * (q % 4)
                    link(nc.vector.tensor_reduce(
                        maxes[0:nt, k:k + QH],
                        BS[q % 2][0:nt, 0:QH * GW].rearrange("p (h n) -> p h n", h=QH)[:, :, 0:nt], AX_X, ALU.max))
                    nc.vector.tensor_scalar(negmax[0:nt, k:k + QH], maxes[0:nt, k:k + QH], -DH ** -0.5, None,
                                            ALU.mult).then_inc(s_max[l], 1)

                def normalise(q):
                    c, g, t = QUADS[q]
                    nt, k = NTOK[g], QH * (q % 4)
                    dve.wait_ge(s_exp[l], QH * (q + 1))
                    link(nc.vector.reciprocal(rsum[0:nt, k:k + QH], sums[0:nt, k:k + QH]))
                    pr = probs[0:nt, q % 4, :].rearrange("p (h n) -> p h n", h=QH)[:, :, 0:nt]
                    rb = rsum[0:nt, k:k + QH].rearrange("p (h n) -> p h n", n=1).to_broadcast([nt, QH, nt])
                    nc.vector.tensor_tensor(pr, pr, rb, ALU.mult).then_inc(p_norm[l], 1)

                def move_t(q):
                    c, g, t = QUADS[q]
                    nt = NTOK[g]
                    dve.wait_ge(t_mm[l], q + 1)
                    if q >= 2:
                        dve.wait_ge(o_mm[l], q - 1)
                    nc.vector.tensor_copy(
                        probsT[0:nt, q % 2, :].rearrange("p (h n) -> p h n", h=QH)[:, :, 0:nt],
                        BT[q % 2][0:nt, 0:QH * GW].rearrange("p (h n) -> p h n", h=QH)[:, :, 0:nt],
                    ).then_inc(t_dve[l], 1)

                def low_out(pair):
                    c, g, t = QUADS[2 * pair]
                    nt, a = NTOK[g], g * GW - CHUNKS[c][0]
                    dve.wait_ge(o_high[l], pair + 1)
                    nc.vector.tensor_tensor(heads_out(1, c, t, a, nt), out_pair(pair, nt),
                                            heads_out(0, c, t, a, nt).bitcast(F32),
                                            ALU.subtract).then_inc(o_low[l], 1)

                def add_out(c):
                    a, w = CHUNKS[c]
                    for dc in range(KD):
                        dve.wait_ge(out_mm[l], KD * c + dc + 1)
                        if l == 0:
                            ins = nc.vector.tensor_tensor(h[:, dc, a:a + w], BD[dc][:, 0:w], h[:, dc, a:a + w],
                                                          ALU.add)
                        else:
                            ins = nc.vector.scalar_tensor_tensor(
                                h[:, dc, a:a + w], BD[dc][:, 0:w], prm[:, S_BO + dc:S_BO + dc + 1],
                                h[:, dc, a:a + w], ALU.add, ALU.add)
                        ins.then_inc(h_attn[l], 1)

                for c in range(NC):
                    for side in qk_sides(l, c):
                        center(*side)
                        finish(*side)
                    mine, steps = quads(c)
                    if c == 0:
                        move_v(0)
                    for q in steps:
                        if q in mine:
                            row_max(q)
                        if q - LAG + 1 in mine:
                            normalise(q - LAG + 1)
                        if q in mine and q % NQ == 3 and q // NQ + 1 < NG:
                            move_v(q // NQ + 1)
                        if q - LAG in mine:
                            move_t(q - LAG)
                        if q - LAG - 1 in mine and (q - LAG - 1) % 2:
                            low_out((q - LAG - 1) // 2)
                    add_out(c)

            attention(0)

            NS = KH * NC

            def ff_find(s):
                v, a, kn, y0, y1 = ff_bufs(s)
                dve.wait_ge(ff_abs, s + 1)
                nc.vector.tensor_scalar(kn, a, -(KNOT - 1) / 2, MAGIC_KNOT, ALU.add, ALU.add).then_inc(ff_knot, 1)
                dve.wait_ge(ff_knot, s + 1)
                nc.vector.scalar_tensor_tensor(a, kn, MAGIC_KNOT, a, ALU.subtract, ALU.subtract).then_inc(ff_frac, 1)

            def ff_interp(s):
                v, a, kn, y0, y1 = ff_bufs(s)
                dve.wait_ge(ff_dy, s + 1)
                dve.wait_ge(ff_frac, s + 1)
                nc.vector.tensor_tensor(a, a, y1, ALU.mult).then_inc(ff_lin, 1)
                dve.wait_ge(ff_lin, s + 1)
                nc.vector.scalar_tensor_tensor(y0, y0, KNOT, a, ALU.mult, ALU.subtract).then_inc(ff_q, 1)

            def ff_store(s):
                v, a, kn, y0, y1 = ff_bufs(s)
                c, m = s // KH, s % KH
                w = CHUNKS[c][1]
                dve.wait_ge(ff_sum, s + 1)
                link(nc.vector.tensor_scalar(y0, y0, UNIT / KNOT, MAGIC, ALU.mult, ALU.add))
                if c >= 2:
                    dve.wait_ge(ff2_mm, KD * (c - 1))
                high, low = (hid[:, c % 2, k, m * CW:m * CW + w] for k in range(2))
                link(nc.vector.tensor_scalar(high, y0, MAGIC, None, ALU.subtract))
                nc.vector.scalar_tensor_tensor(low, y0, MAGIC, high.bitcast(F32), ALU.subtract,
                                               ALU.subtract).then_inc(ff_hid, 1)

            def ff_out(c):
                a, w = CHUNKS[c]
                for dc in range(KD):
                    dve.wait_ge(ff2_mm, KD * c + dc + 1)
                    t = rt[:, 0:w]
                    nc.vector.tensor_scalar(t, BO[dc][:, 0:w], b2u[:, dc:dc + 1], MAGIC, ALU.add,
                                            ALU.add).then_inc(ff2_ev, 1)
                    dve.wait_ge(ff2_ev, KD * c + dc + 1)
                    link(nc.vector.tensor_scalar(t, t, MAGIC, 1.0 / UNIT, ALU.subtract, ALU.mult))
                    nc.vector.tensor_tensor(h[:, dc, a:a + w], h[:, dc, a:a + w], t, ALU.add).then_inc(h_ff, 1)
                    dve.wait_ge(h_ff, KD * c + dc + 1)

            center(1, 3)
            for s in range(NS + 2):
                if s < NS:
                    ff_find(s)
                if 1 <= s <= NS:
                    ff_interp(s - 1)
                if s >= 2:
                    ff_store(s - 2)
                if s == 4:
                    finish(1, 3)
                if 2 * KH <= s < NS and s % KH == 4:
                    ff_out(s // KH - 2)
                if s == 2 * KH + 6:
                    center(2, 0)
            finish(2, 0)
            ff_out(NC - 2)
            ff_out(NC - 1)
            attention(1)
            center(3, 3)
            dve.wait_ge(o_mm[1], len(QUADS))
            for t, value in ((logits, BIG), (keys, BIG), (gates, 0.0)):
                last = tick(nc.vector.memset(t, value))
            dve.wait_ge(dve_line, last)

            full = (NG - 1) * E

            def start_search():
                dve.wait_ge(log_mm, NG)
                link(nc.vector.tensor_copy(logits[0:NTOK[0], 0:full], BO[0][0:NTOK[0], 0:full]))
                link(nc.vector.tensor_copy(logits[0:NTOK[-1], full:], BO[0][0:NTOK[-1], full:NG * E]))
                link(nc.vector.memset(found[:, :], 0))

            def search(i):
                if i > 0:
                    judge(i - 1)
                if i == 32:
                    return
                if i > 0:
                    bit = 31 - i
                    link(nc.vector.tensor_scalar(tryb[:, :], found[:, :], 1 << bit, None, ALU.bitwise_or))
                src, than = (logits, 0.0) if i == 0 else (keys, tryb[:, 0:1].bitcast(F32))
                nc.vector.tensor_scalar(below, src[:, :], than, None, ALU.is_lt, ALU.add,
                                        accum_out=count[:, i % 2:i % 2 + 1]).then_inc(cnt_ready, 1)

            def judge(i):
                bit = 31 - i
                dve.wait_ge(cnt_mm, i + 1)
                total = BT[1][:, 0:1]
                if i == 0:
                    link(nc.vector.tensor_scalar(sign[:, :], total, TOPK / D, -2.0, ALU.is_ge, ALU.mult))
                    link(nc.vector.tensor_scalar(sign[:, :], sign[:, :], 1.0, None, ALU.add))
                    link(nc.vector.tensor_scalar(rank[:, :], sign[:, :], (2 * TOPK - NLOG - 1) / (2 * D),
                                                 (NLOG + 1) / (2 * D), ALU.mult, ALU.add))
                    for rows, a, b in ((NTOK[0], 0, full), (NTOK[-1], full, NG * E)):
                        link(nc.vector.tensor_scalar(keys[0:rows, a:b], logits[0:rows, a:b], sign[0:rows, 0:1],
                                                     None, ALU.mult))
                else:
                    link(nc.vector.tensor_scalar(newb[:, :], total, rank[:, 0:1], float(1 << bit), ALU.is_lt,
                                                 ALU.mult))
                    link(nc.vector.tensor_tensor(found[:, :], found[:, :], newb[:, :], ALU.bitwise_or))

            def gate():
                link(nc.vector.tensor_scalar(kth[:, :], found[:, :].bitcast(F32), sign[:, 0:1], None, ALU.mult))
                link(nc.vector.scalar_tensor_tensor(gates[0:NTOK[0], 0:full], logits[0:NTOK[0], 0:full],
                                                    kth[0:NTOK[0], 0:1], logits[0:NTOK[0], 0:full],
                                                    ALU.is_ge, ALU.mult))
                nc.vector.scalar_tensor_tensor(gates[0:NTOK[-1], full:], logits[0:NTOK[-1], full:],
                                               kth[0:NTOK[-1], 0:1], logits[0:NTOK[-1], full:],
                                               ALU.is_ge, ALU.mult).then_inc(gates_ready, 1)

            def moe_split(s):
                c, m = s // KH % NC, s % KH
                w = CHUNKS[c][1]
                j = s // KH
                dve.wait_ge(m_gelu, s + 1)
                if j >= 2:
                    dve.wait_ge(m2_mm, KD * (j - 1))
                high, low = (hid[:, j % 2, k, m * CW:m * CW + w] for k in range(2))
                nc.vector.tensor_copy(high, moe_g(s)[:, 0:w]).then_inc(m_high, 1)
                dve.wait_ge(m_high, s + 1)
                nc.vector.tensor_tensor(low, moe_g(s)[:, 0:w], high.bitcast(F32), ALU.subtract).then_inc(m_hid, 1)

            def moe_out(e, c):
                for dc in range(KD):
                    moe_out1(e, c, dc)

            def moe_out1(e, c, dc):
                w = CHUNKS[c][1]
                if True:
                    j = (e * NC + c) * KD + dc
                    dve.wait_ge(m2_mm, j + 1)
                    if e == 0:
                        nc.vector.tensor_scalar(moe_y0(j)[:, 0:w], BO[dc][:, 0:w],
                                                prm[:, S_B2M + dc * E:S_B2M + dc * E + 1], None,
                                                ALU.add).then_inc(m_y, 1)
                        return
                    dve.wait_ge(gb_act, e * NC + c + 1)
                    dve.wait_ge(h_moe, max(j - 3, 1))
                    nc.vector.scalar_tensor_tensor(
                        moe_y(j)[:, 0:w], BO[dc][:, 0:w], prm[:, S_B2M + dc * E + e:S_B2M + dc * E + e + 1],
                        moe_gate(e, c)[:, 0:w], ALU.add, ALU.mult).then_inc(m_y, 1)

            steps = [(e, c) for e in range(E) for c in range(NC)]
            for s in range(E * NC * KH):
                n, m = s // KH, s % KH
                moe_split(s)
                if s == 5:
                    finish(3, 3)
                if s == KH - 1:
                    start_search()
                if m % 2 == 0 and 1 <= n <= 4:
                    search(8 * (n - 1) + m // 2)
                if m == KH - 1 and 1 <= n <= 4:
                    for i in range(4, 8):
                        search(8 * (n - 1) + i)
                        if i % 2:
                            moe_out1(*steps[n - 1], (i - 4) // 2)
                if n == 5 and m == 1:
                    search(32)
                    gate()
                if s % KH == 4 and s >= (NC + 2) * KH:
                    moe_out(*steps[s // KH - 2])
            moe_out(*steps[-2])
            moe_out(*steps[-1])


def layout(i):
    import numpy as np

    def rows(a):
        k = a.shape[0] // P
        return a.reshape(k, P, -1).transpose(1, 0, 2).reshape(P, -1)

    i = {k: np.asarray(v) for k, v in i.items()}
    col = np.array([g * GW + t for g in range(NG) for t in range(NTOK[g])])
    patch = np.array([c for n, c in enumerate(col) if n % TOK])
    px = i["x"].reshape(B, C, SIDE, PATCH, SIDE, PATCH).transpose(1, 3, 5, 0, 2, 4).reshape(C * PATCH * PATCH, -1)
    xt = np.zeros((C * PATCH * PATCH, T), np.float32)
    xt[:, patch] = px
    a = {"x": xt.reshape(KF, P, T).transpose(1, 0, 2), "w_lin": rows(i["L0_tok_W_lin"].T)}
    a["attn0"] = np.stack([rows(i[f"L0_attn_w{n}"].reshape(HD, D).T) for n in "qkv"]
                          + [rows(i["L0_attn_wo"].T)])
    a["ffn"] = np.stack([rows(i["L0_ffn_w1"]), rows(i["L0_ffn_w2"])])
    a["attn1"] = np.stack([rows(i[f"L1_attn_W{n}"]) for n in "qkvo"])
    w1, w2 = i["L1_ffn_w1"], i["L1_ffn_w2"]
    a["moe"] = np.stack([rows(w.T) for e in range(E) for w in (w1[e], w2[e])])
    a["small"] = np.concatenate(
        [rows(i["L0_tok_position_embeddings"][0].T)]
        + [rows(v.reshape(-1, 1)) for v in (i["L0_tok_class_token"], i["L0_tok_b_lin"], i["L1_attn_bo"],
                                            i["L0_ffn_b1"], i["L0_ffn_b2"])]
        + [rows(i["L1_ffn_b1"][e].reshape(-1, 1)) for e in range(E)]
        + [rows(i["L1_ffn_b2"].T), rows(i["L1_ffn_gate_weight"].T)], axis=1)
    t = np.arange(P)
    same = (t[:, None] // TOK == t[None, :] // TOK)[:, :GW]
    late = (t[None, :] > t[:, None])[:, :GW]
    a["b1"] = i["L0_ffn_b1"].reshape(1, FF)
    a["ident"] = np.eye(P, dtype=np.float32)
    a["mask"] = np.stack([np.where(same & ~late, 0.0, -1e30), np.where(same, 0.0, -1e30)],
                         axis=1).astype(np.float32)
    return {f"in_{k}": np.ascontiguousarray(v) for k, v in a.items()}, col


def kernel(**inputs):
    import concourse.bacc as bacc
    from concourse.bass_utils import run_bass_kernel_spmd

    arrays, col = layout(inputs)
    nc = bacc.Bacc("TRN2", target_bir_lowering=False, num_devices=1)
    args = {n: nc.dram_tensor(n, a.shape, F32, kind="ExternalInput").ap() for n, a in arrays.items()}
    out = nc.dram_tensor("out", (P, KD, T), F32, kind="ExternalOutput").ap()
    weights = [args[f"in_{name}"][i] for name in ("attn0", "ffn", "attn1", "moe")
               for i in range(arrays[f"in_{name}"].shape[0])]
    vit_tower(nc, args["in_x"], args["in_w_lin"], weights, args["in_small"], args["in_ident"],
              args["in_mask"], args["in_b1"], out)
    r = run_bass_kernel_spmd(nc, [arrays], core_ids=[0])
    got = r.results[0]["out"]
    return got.transpose(2, 1, 0).reshape(T, D)[col].reshape(B, TOK, D)
```

```python
from contextlib import ExitStack

import concourse.bass as bass
from concourse import mybir

F32 = mybir.dt.float32
F32R = mybir.dt.float32r
BF16 = mybir.dt.bfloat16
I32 = mybir.dt.int32
ALU = mybir.AluOpType
ACT = mybir.ActivationFunctionType
AX_X = mybir.AxisListType.X

P = 128
B, C, IMG, PATCH = 32, 3, 96, 16
SIDE = IMG // PATCH
TOK = SIDE * SIDE + 1
D = 256
KD = D // P
KF = C * PATCH * PATCH // P
HEADS, DH = 16, 64
HD = HEADS * DH
KO = HD // P
FF = 1024
KH = FF // P
E = 8
TOPK = 4 * 256 * 6
NLOG = B * TOK * E

GI = 3
GW = GI * TOK + 1
NG = -(-B // GI)
NTOK = [min(GI, B - g * GI) * TOK for g in range(NG)]
T = (NG - 1) * GW + NTOK[-1]
VLAG = 2
LAG = 3
GC = 3
CW = GC * GW
NC = -(-NG // GC)
CHUNKS = [(c * CW, min(CW, T - c * CW)) for c in range(NC)]
MW = 2 * -(-T // (2 * NC))
MCHUNKS = [(c * MW, min(MW, T - c * MW)) for c in range(NC)]
GROUPS = [list(range(c * GC, min((c + 1) * GC, NG))) for c in range(NC)]
QH = 4
NQ = HEADS // QH
QUADS = [(c, g, t) for c in range(NC) for g in GROUPS[c] for t in range(NQ)]

EPS = 1e-5
UNIT = 256.0
MAGIC = 1.5 * 2.0 ** 23
KNOT = 64.0
MAGIC_KNOT = MAGIC * KNOT
BL = 32
BIG = 3.4028234663852886e38

S_POS = 0
S_CLS = S_POS + KD * TOK
S_BLIN = S_CLS + KD
S_BO = S_BLIN + KD
S_B1F = S_BO + KD
S_B2F = S_B1F + KH
S_B1M = S_B2F + KD
S_B2M = S_B1M + E * KH
S_GATE = S_B2M + KD * E
S_END = S_GATE + KD * E

SPLITS = 4
NP = KH * NC // 2
PIECE = KD * 1024
WSLOTS = 4


def vit_tower(nc, x, w_lin, weights, small, ident_in, mask_in, b1_in, out):
    with ExitStack() as ctx:
        def sb(name, shape, dt=F32):
            return ctx.enter_context(nc.sbuf_tensor(name, shape, dt))

        def sem(name):
            return ctx.enter_context(nc.semaphore(name))

        h = sb("h", [P, KD, T])
        xn = sb("xn", [P, 2, KD, T], F32R)
        wslot = sb("wslot", [P, WSLOTS, 2, PIECE], F32R)
        raw = sb("raw", [P, 2, PIECE])
        hid = sb("hid", [P, 2, 2, KH * CW], F32R)
        work = sb("work", [P, HEADS, CW])
        vbuf = sb("vbuf", [P, 2, HD])
        probs = sb("probs", [P, 4, QH * GW])
        probsT = sb("probsT", [P, 2, QH * GW])
        xc = sb("xc", [P, KD, CW])
        sq = sb("sq", [P, KD, CW])
        rs = sb("rs", [P, CW])
        rt = sb("rt", [P, CW])
        prm = sb("prm", [P, S_END])
        addT = sb("addT", [P, KD, TOK])
        b1r = sb("b1r", [BL + 1, FF], F32R)
        ones_r = sb("ones_r", [BL + 1, CW], F32R)
        b2u = sb("b2u", [P, KD])
        gateR = sb("gateR", [P, 2, KD * E], F32R)
        ident = sb("ident", [P, P])
        identb = sb("identb", [P, P], BF16)
        maskb = sb("maskb", [P, 2, QH, GW], BF16)
        mean_w = sb("mean_w", [P, P])
        c_eps = sb("c_eps", [P, 1])
        c_magic = sb("c_magic", [P, 2])
        c_knot0 = sb("c_knot0", [P, 1])
        c_knot1 = sb("c_knot1", [P, 1])
        negmax = sb("negmax", [P, 4 * QH])
        maxes = sb("maxes", [P, 4 * QH])
        sums = sb("sums", [P, 4 * QH])
        rsum = sb("rsum", [P, 4 * QH])
        count = sb("count", [P, 2])
        sign = sb("sign", [P, 1])
        rank = sb("rank", [P, 1])
        kth = sb("kth", [P, 1])
        found = sb("found", [P, 1], I32)
        tryb = sb("tryb", [P, 1], I32)
        newb = sb("newb", [P, 1], I32)

        logits, keys, below, gates = (probsT[:, 0, i * NG * E:(i + 1) * NG * E] for i in range(4))
        maskf = probsT[:, 1, 0:2 * GW].rearrange("p (l n) -> p l n", l=2)
        b1row = probs[0:BL + 1, :, :].rearrange("p s n -> p (s n)")[:, 0:FF]

        bank = {n: ctx.enter_context(nc.psum_tensor(n, [P, 512], F32))
                for n in ("D0", "D1", "S0", "S1", "T0", "T1", "O0", "O1")}
        BD = [bank["D0"], bank["D1"]]
        BS = [bank["S0"], bank["S1"]]
        BT = [bank["T0"], bank["T1"]]
        BO = [bank["O0"], bank["O1"]]
        BH = BD + BS

        small_in = sem("small_in")
        mats_in = sem("mats_in")
        raw_in = [sem("raw_in0"), sem("raw_in1")]
        patch_in = [sem(f"patch_in{n}") for n in range(NC - 1)]
        high_ready = sem("high_ready")
        start_split = sem("start_split")
        pool_split = sem("pool_split")
        dve_line = sem("dve_line")
        pool_part = sem("pool_part")
        consts = sem("consts")
        params = sem("params")
        masks = sem("masks")
        b1_ready = sem("b1_ready")
        emb_mm = sem("emb_mm")
        h_set = sem("h_set")
        ln_mean = [sem(f"ln_mean{n}") for n in range(4)]
        ln_xc = [sem(f"ln_xc{n}") for n in range(4)]
        ln_sq = [sem(f"ln_sq{n}") for n in range(4)]
        ln_var = [sem(f"ln_var{n}") for n in range(4)]
        ln_ln = [sem(f"ln_ln{n}") for n in range(4)]
        ln_rs = [sem(f"ln_rs{n}") for n in range(4)]
        ln_out = [sem(f"ln_out{n}") for n in range(4)]
        qk_mm = [sem(f"qk_mm{n}") for n in range(2)]
        qk_act = [sem(f"qk_act{n}") for n in range(2)]
        v_mm = [sem(f"v_mm{n}") for n in range(2)]
        v_act = [sem(f"v_act{n}") for n in range(2)]
        v_dve = [sem(f"v_dve{n}") for n in range(2)]
        s_mm = [sem(f"s_mm{n}") for n in range(2)]
        s_max = [sem(f"s_max{n}") for n in range(2)]
        s_exp = [sem(f"s_exp{n}") for n in range(2)]
        s_inv = [sem(f"s_inv{n}") for n in range(2)]
        p_norm = [sem(f"p_norm{n}") for n in range(2)]
        t_mm = [sem(f"t_mm{n}") for n in range(2)]
        t_dve = [sem(f"t_dve{n}") for n in range(2)]
        o_mm = [sem(f"o_mm{n}") for n in range(2)]
        o_high = [sem(f"o_high{n}") for n in range(2)]
        o_low = [sem(f"o_low{n}") for n in range(2)]
        out_mm = [sem(f"out_mm{n}") for n in range(2)]
        h_attn = [sem(f"h_attn{n}") for n in range(2)]
        ff1_mm = sem("ff1_mm")
        ff_t = sem("ff_t")
        ff_abs = sem("ff_abs")
        ff_knot = sem("ff_knot")
        ff_y0 = sem("ff_y0")
        ff_y1 = sem("ff_y1")
        ff_dy = sem("ff_dy")
        ff_frac = sem("ff_frac")
        ff_lin = sem("ff_lin")
        y0_gated = sem("y0_gated")
        ff_q = sem("ff_q")
        ff_pos = sem("ff_pos")
        ff_z = sem("ff_z")
        ff_hi = sem("ff_hi")
        ff_hid = sem("ff_hid")
        ff2_mm = sem("ff2_mm")
        ff2_ev = sem("ff2_ev")
        h_ff = sem("h_ff")
        log_mm = sem("log_mm")
        cnt_ready = sem("cnt_ready")
        cnt_mm = sem("cnt_mm")
        gates_ready = sem("gates_ready")
        gb_mm = sem("gb_mm")
        gb_act = sem("gb_act")
        m1_mm = sem("m1_mm")
        m_gelu = sem("m_gelu")
        m_high = sem("m_high")
        m_hid = sem("m_hid")
        m2_mm = sem("m2_mm")
        m_y = sem("m_y")
        h_moe = sem("h_moe")
        stored = sem("stored")

        FIRST_W = 1 + NC
        NSTART = FIRST_W + 1
        NPIECE = FIRST_W + len(weights)

        def piece_split(i):
            return (start_split, i + 1) if i < NSTART else (pool_split, i - NSTART + 1)

        def piece_place(i):
            if i == 0:
                return [wslot[:, WSLOTS - 1, k, 0:KF * D] for k in range(2)]
            if i < FIRST_W:
                c = i - 1
                return [hid[:, c % 2, k, 0:KF * CHUNKS[c][1]] for k in range(2)]
            return [wslot[:, (i - FIRST_W) % WSLOTS, k, :] for k in range(2)]

        def piece_raw(i):
            if 2 <= i <= 3:
                n = KF * CW
                return work[:, :, :].rearrange("p m n -> p (m n)")[:, (i - 2) * n:(i - 2) * n + piece_size(i)]
            if i == 4:
                return vbuf[:, :, :].rearrange("p s n -> p (s n)")[:, 0:piece_size(i)]
            return raw[:, (i if i < 2 else i - 3) % 2, 0:piece_size(i)]

        def landed(eng, i):
            if 2 <= i <= 4:
                eng.wait_ge(patch_in[i - 2], 16)
            else:
                k = i if i < 2 else i - 3
                eng.wait_ge(raw_in[k % 2], 16 * (k // 2 + 1))

        def piece_size(i):
            return KF * D if i == 0 else KF * CHUNKS[i - 1][1] if i < FIRST_W else PIECE

        def place_free(i):
            if i < FIRST_W:
                return (emb_mm, KD * (i - 2)) if i >= 3 else None
            j = i - FIRST_W
            if j < WSLOTS - 1:
                return None
            return [(emb_mm, KD * NC),
                    (qk_mm[0], 16 * (NC - 1) + 8), (qk_mm[0], 16 * NC), (v_mm[0], 2 * NG), (out_mm[0], KD * NC),
                    (ff1_mm, KH * NC), (ff2_mm, KD * NC),
                    (qk_mm[1], 16 * (NC - 1) + 8), (qk_mm[1], 16 * NC), (v_mm[1], 2 * NG), (out_mm[1], KD * NC),
                    ][j - 3] if j < 14 else ((m1_mm, m2_mm)[j % 2], (KH, KD)[j % 2] * NC * ((j - 14) // 2 + 1))

        W_QKVO = [0, 6]
        W_FF, W_MOE = 4, 10

        def weight(j, k, width):
            return wslot[:, j % WSLOTS, k, :].rearrange("p (a n) -> p a n", n=width)

        def wait_weight(eng, j):
            eng.wait_ge(*piece_split(FIRST_W + j))

        def heads(t):
            return [2 * QH * (t // 2) + t % 2 + 2 * i for i in range(QH)]

        def cols(g):
            return slice(g * GW, g * GW + NTOK[g])

        def ff_bufs(p):
            w = CHUNKS[2 * p // KH][1]
            if p % 3 < 2:
                four = [work[:, 8 * (p % 3) + 2 * k:8 * (p % 3) + 2 * k + 2, :] for k in range(4)]
            else:
                flat = vbuf[:, :, :].rearrange("p s n -> p (s n)")
                four = [t.rearrange("p (i n) -> p i n", i=2) for t in
                        [flat[:, 2 * k * CW:2 * (k + 1) * CW] for k in range(3)]
                        + [probs[:, :, :].rearrange("p s n -> p (s n)")[:, 0:2 * CW]]]
            return [t[:, :, 0:w] for t in four]

        def ff_rows(p, k):
            c, m = 2 * p // KH, 2 * p % KH
            return hid[:, c % 2, k, :].rearrange("p (m n) -> p m n", n=CW)[:, m:m + 2, 0:CHUNKS[c][1]]

        def moe_add(pool, e, c, dc):
            a, w = MCHUNKS[c]
            j = (e * NC + c) * KD + dc
            pool.wait_ge(m_y, j + 1)
            if j >= KD * NC:
                pool.wait_ge(h_moe, j - KD * NC + 1)
            nc.gpsimd.tensor_tensor(h[:, dc, a:a + w], h[:, dc, a:a + w], moe_y(j)[:, 0:w],
                                    ALU.add).then_inc(h_moe, 1)

        def moe_first(pool, j):
            c, dc = j // KD, j % KD
            a, w = MCHUNKS[c]
            pool.wait_ge(gb_act, c + 1)
            pool.wait_ge(m_y, j + 1)
            y = moe_y0(j)[:, 0:w]
            nc.gpsimd.tensor_tensor(y, y, moe_gate(0, c)[:, 0:w], ALU.mult).then_inc(y0_gated, 1)
            pool.wait_ge(y0_gated, j + 1)
            nc.gpsimd.tensor_tensor(h[:, dc, a:a + w], h[:, dc, a:a + w], y, ALU.add).then_inc(h_moe, 1)

        def moe_y0(j):
            return vbuf[:, j // 3, j % 3 * CW:(j % 3 + 1) * CW] if j < 6 else probs[:, j - 6, 0:CW]

        def moe_g(s):
            return work[:, s % 4, :]

        def moe_y(j):
            return work[:, 4 + j % 4, :]

        def moe_gate(e, c):
            return work[:, 8 + (e % 2) * NC + c, :]

        def heads_out(k, c, t, a, nt):
            m = QH * (t // 2)
            return hid[:, c % 2, k, :].rearrange("p (m n) -> p m n", n=CW)[:, m:m + QH, a:a + nt]

        def out_pair(pair, nt):
            return BO[pair % 2][:, 0:QH * GW].rearrange("p (m n) -> p m n", n=GW)[:, :, 0:nt]

        def quads(c):
            mine = [q for q in range(len(QUADS)) if QUADS[q][0] == c]
            tail = LAG + VLAG
            n = 2 * KO // tail
            steps = [(q, None, ()) for q in mine]
            for k in range(tail):
                ms = range(k * n, (k + 1) * n if k < tail - 1 else 2 * KO) if c + 1 < NC else ()
                steps.append((mine[-1] + 1 + k, k, ms))
            return mine, steps

        def qk_sides(l, c):
            if c == 0:
                sides = [(2 * l, i) for i in range(2 - l, NC)]
                return {5 * k: v for k, v in enumerate(sides)}, {5 * k + 4: v for k, v in enumerate(sides)}
            if c == 1:
                return {}, {}
            return {2 * KO - 4: (2 * l + 1, c - 2)}, {2 * KO - 1: (2 * l + 1, c - 2)}

        block = ctx.enter_context(nc.Block())

        @block.sync
        def _(sp):
            for i in range(NPIECE):
                if i == FIRST_W or i == FIRST_W + 1:
                    sp.wait_ge(*piece_split(i - FIRST_W))
                elif i > FIRST_W + 1:
                    sp.wait_ge(*piece_split(i - 2))
                if i == 0:
                    src = w_lin
                elif i < FIRST_W:
                    a, w = CHUNKS[i - 1]
                    src = x[:, :, a:a + w]
                else:
                    src = weights[i - FIRST_W]
                dst = piece_raw(i)
                if 0 < i < FIRST_W:
                    dst = dst.rearrange("p (k n) -> p k n", k=KF)
                sp.dma_start(dst, src).then_inc(patch_in[i - 2] if 2 <= i <= 4 else raw_in[(i if i < 2 else i - 3) % 2], 16)
                if i == 1:
                    sp.dma_start(prm[:, :], small).then_inc(small_in, 16)
                    sp.dma_start(ident[:, :], ident_in).then_inc(mats_in, 16)
                    sp.dma_start(maskf, mask_in).then_inc(mats_in, 16)
                    sp.dma_start(b1row[0:1, :], b1_in).then_inc(mats_in, 16)
                    sp.dma_start(b1row[BL:BL + 1, :], b1_in).then_inc(mats_in, 16)
            for c, (a, w) in enumerate(MCHUNKS):
                sp.wait_ge(h_moe, KD * NC * (E - 1) + KD * (c + 1))
                sp.dma_start(out[:, :, a:a + w], h[:, :, a:a + w]).then_inc(stored, 16)
            sp.wait_ge(stored, 16 * NC)

        @block.gpsimd
        def _(pool):
            nc.gpsimd.memset(mean_w[:, :], 1.0 / D).then_inc(consts, 1)
            nc.gpsimd.memset(c_eps[:, :], EPS).then_inc(consts, 1)
            nc.gpsimd.memset(ones_r[:, :].bitcast(F32), 1.0).then_inc(consts, 1)
            nc.gpsimd.memset(b1r[:, :].bitcast(F32), 0.0).then_inc(consts, 1)
            for k, value in enumerate((MAGIC, -MAGIC)):
                nc.gpsimd.memset(c_magic[:, k:k + 1], value).then_inc(consts, 1)
            nc.gpsimd.memset(c_knot0[:, :], MAGIC_KNOT / UNIT).then_inc(consts, 1)
            nc.gpsimd.memset(c_knot1[:, :], (MAGIC_KNOT - KNOT) / UNIT).then_inc(consts, 1)

            def split(i):
                pool.wait_ge(high_ready, i + 1)
                high, low = piece_place(i)
                nc.gpsimd.tensor_tensor(low, piece_raw(i), high.bitcast(F32), ALU.subtract).then_inc(pool_split, 1)

            def split_part(i, k):
                pool.wait_ge(high_ready, i + 1)
                high, low = piece_place(i)
                sl = slice(k * PIECE // SPLITS, (k + 1) * PIECE // SPLITS)
                nc.gpsimd.tensor_tensor(low[:, sl], piece_raw(i)[:, sl], high.bitcast(F32)[:, sl],
                                        ALU.subtract).then_inc(pool_split if k == SPLITS - 1 else pool_part, 1)

            def normalise(l):
                for q in range(len(QUADS)):
                    c, g, t = QUADS[q]
                    nt, k = NTOK[g], QH * (q % 4)
                    pr = probs[0:nt, q % 4, :].rearrange("p (h n) -> p h n", h=QH)[:, :, 0:nt]
                    rb = rsum[0:nt, k:k + QH].rearrange("p (h n) -> p h n", n=1).to_broadcast([nt, QH, nt])
                    pool.wait_ge(s_inv[l], q + 1)
                    nc.gpsimd.tensor_tensor(pr, pr, rb, ALU.mult).then_inc(p_norm[l], 1)
                    k = q - (len(QUADS) - 2 * SPLITS)
                    if k >= 0:
                        split_part(FIRST_W + W_QKVO[l] + 4 + k // SPLITS, k % SPLITS)

            for i in range(NSTART, FIRST_W + W_FF):
                split(i)
            normalise(0)
            for p in range(NP):
                if KH // 2 < p <= 3 * KH // 2:
                    k = p - KH // 2 - 1
                    split_part(FIRST_W + W_FF + 2 + k // SPLITS, k % SPLITS)
                v, a, y1, y0 = ff_bufs(p)
                pool.wait_ge(ff_y1, p + 1)
                nc.gpsimd.tensor_tensor(y1, y1, y0, ALU.subtract).then_inc(ff_dy, 1)
                pool.wait_ge(ff_dy, p + 1)
                nc.gpsimd.tensor_tensor(a, a, y1, ALU.mult).then_inc(ff_lin, 1)
            for i in range(FIRST_W + W_MOE - 2, FIRST_W + W_MOE):
                split(i)
            normalise(1)
            for i in range(FIRST_W + W_MOE + 2, FIRST_W + W_MOE + 4):
                split(i)
            for e in range(1, E):
                for c in range(NC):
                    if c == 0 and e + 1 < E:
                        for i in (2, 3):
                            split(FIRST_W + W_MOE + 2 * e + i)
                    if e == 1 and c == 0:
                        for j in range(KD * NC):
                            moe_first(pool, j)
                    for dc in range(KD):
                        moe_add(pool, e, c, dc)

        def split_products(pe, psum, w, xs, n, last_sem, between=None, first=True):
            k = 0
            for i in range(n):
                (wh, wl), (xh, xl) = w(i), xs(i)
                for a, b in ((wh, xh), (wh, xl), (wl, xh)):
                    mm = pe.matmul(psum, a, b, start=(first and k == 0), stop=(k == 3 * n - 1))
                    k += 1
                if between is not None and i == n // 2 - 1:
                    between()
            mm.then_inc(last_sem, 1)

        @block.tensor
        def _(pe):
            def hidden(slot, kk, a, w):
                return [hid[:, slot, k, kk * CW + a:kk * CW + a + w] for k in range(2)]

            def normed(kk, sl):
                return [xn[:, k, kk, sl] for k in range(2)]

            def embed(c):
                a, w = CHUNKS[c]
                pe.wait_ge(*piece_split(1 + c))
                for dc in range(KD):
                    if c >= 1:
                        pe.wait_ge(h_set, KD * (c - 1) + dc + 1)
                    wl = [wslot[:, WSLOTS - 1, k, 0:KF * D].rearrange("p (a n) -> p a n", n=D) for k in range(2)]
                    split_products(pe, BD[dc][:, 0:w],
                                   lambda i: [t[:, i, dc * P:(dc + 1) * P] for t in wl],
                                   lambda i: [hid[:, c % 2, k, i * w:(i + 1) * w] for k in range(2)],
                                   KF, emb_mm)

            NORMED = [h_set, h_attn[0], h_ff, h_attn[1]]

            def mean(n, c):
                a, w = CHUNKS[c]
                pe.wait_ge(NORMED[n], KD * (c + 1))
                if c >= 1:
                    pe.wait_ge(ln_xc[n], c)
                for k in range(KD):
                    mm = pe.matmul(BT[0][:, 0:w], mean_w[:, :], h[:, k, a:a + w],
                                   start=(k == 0), stop=(k == KD - 1))
                mm.then_inc(ln_mean[n], 1)

            def variance(n, c):
                a, w = CHUNKS[c]
                pe.wait_ge(ln_sq[n], c + 1)
                if c >= 1:
                    pe.wait_ge(ln_out[n], c)
                for k in range(KD):
                    mm = pe.matmul(BT[1][:, 0:w], mean_w[:, :], sq[:, k, 0:w],
                                   start=(k == 0), stop=(k == KD - 1))
                mm.then_inc(ln_var[n], 1)

            def attention(l, n):
                q_w, k_w, v_w, o_w = (W_QKVO[l] + i for i in range(4))

                def project_qk(c, ms):
                    if not ms:
                        return
                    a, w = CHUNKS[c]
                    means, variances = qk_sides(l, c)
                    if 0 in ms:
                        pe.wait_ge(ln_out[n], c + 1)
                    for m in ms:
                        j = 2 * KO * c + m
                        wj = (q_w, k_w)[m // KO]
                        if c == 0 and m % KO == 0:
                            wait_weight(pe, wj)
                        if m >= 4:
                            pe.wait_ge(qk_act[l], j - 3)
                        elif m < 2 and c >= 1:
                            pe.wait_ge((v_act, v_dve)[m][l], GROUPS[c - 1][-1] + 1)
                        elif c >= 1:
                            pe.wait_ge(s_exp[l], QH * (quads(c - 1)[0][-1] + m - 2))
                        elif m < 2 and l == 0:
                            pe.wait_ge(h_set, KD * (NC - 1) + m + 1)
                        elif l == 1 and c == 0:
                            pe.wait_ge(ff_t, KH * NC - 3 + m)
                        mc = m % KO
                        split_products(pe, BH[m % 4][:, 0:w],
                                       lambda i: [weight(wj, k, HD)[:, i, mc * P:(mc + 1) * P] for k in range(2)],
                                       lambda i: normed(i, slice(a, a + w)), KD, qk_mm[l])
                        if m in means:
                            if c >= 1:
                                pe.wait_ge(t_dve[l], quads(c - 1)[0][-1] + 1)
                            mean(*means[m])
                        if m in variances:
                            variance(*variances[m])

                def project_v(g):
                    if g == 0:
                        wait_weight(pe, v_w)
                    c = g // GC
                    for half in range(2):
                        if g == 0:
                            pe.wait_ge(qk_act[l], 2 * KO - 3 + half)
                        elif g % GC == 0:
                            pe.wait_ge(h_attn[l], KD * (c - 1) + half + 1)
                        else:
                            pe.wait_ge((v_act, v_dve)[half][l], g)
                        split_products(pe, BD[half][0:NTOK[g], :],
                                       lambda i: normed(i, cols(g)),
                                       lambda i: [weight(v_w, k, HD)[:, i, half * 512:(half + 1) * 512]
                                                  for k in range(2)], KD, v_mm[l])

                def scores(q):
                    c, g, t = QUADS[q]
                    nt, a = NTOK[g], g * GW - CHUNKS[c][0]
                    if q == 0:
                        pe.wait_ge(masks, 2)
                        pe.wait_ge(mats_in, 64)
                    if t == 0 and g % GC == 0:
                        pe.wait_ge(qk_act[l], 2 * KO * (c + 1))
                    if q >= 2:
                        pe.wait_ge(s_exp[l], QH * (q - 1))
                    bank4 = BS[q % 2][0:nt, 0:QH * GW].rearrange("p (h n) -> p h n", h=QH)[:, :, 0:nt]
                    pe.matmul(bank4, identb[0:nt, 0:nt], maskb[0:nt, l, :, 0:nt], start=True, stop=False,
                              skip_group_check=True)
                    r = DH * (t % 2)
                    for i, hd in enumerate(heads(t)):
                        mm = pe.matmul(BS[q % 2][0:nt, i * GW:i * GW + nt],
                                       work[r:r + DH, hd // 2, a:a + nt], work[r:r + DH, KO + hd // 2, a:a + nt],
                                       start=False, stop=(i == QH - 1), skip_group_check=True)
                    mm.then_inc(s_mm[l], 1)

                def transposes(q):
                    c, g, t = QUADS[q]
                    nt = NTOK[g]
                    pe.wait_ge(p_norm[l], q + 1)
                    if t == 0 and g % GC == 0 and qk_sides(l, c)[0]:
                        norm, chunk = list(qk_sides(l, c)[0].values())[-1]
                        pe.wait_ge(ln_out[norm], chunk + 1)
                    if q >= 2:
                        pe.wait_ge(t_dve[l], q - 1)
                    for i in range(QH):
                        mm = pe.transpose(BT[q % 2][0:nt, i * GW:i * GW + nt],
                                          probs[0:nt, q % 4, i * GW:i * GW + nt], ident[0:nt, 0:nt])
                    mm.then_inc(t_mm[l], 1)

                def values(q):
                    c, g, t = QUADS[q]
                    nt = NTOK[g]
                    pe.wait_ge(t_dve[l], q + 1)
                    if t == 0:
                        pe.wait_ge(v_act[l], g + 1)
                        pe.wait_ge(v_dve[l], g + 1)
                    if q >= 4:
                        pe.wait_ge(o_low[l], q // 2 - 1)
                    r = DH * (t % 2)
                    for i, hd in enumerate(heads(t)):
                        mm = pe.matmul(BO[q // 2 % 2][r:r + DH, i * GW:i * GW + nt],
                                       vbuf[0:nt, g % 2, hd * DH:(hd + 1) * DH],
                                       probsT[0:nt, q % 2, i * GW:i * GW + nt], start=True, stop=True,
                                       skip_group_check=True)
                    mm.then_inc(o_mm[l], 1)

                def project_out(c):
                    a, w = CHUNKS[c]
                    if c == 0:
                        wait_weight(pe, o_w)
                    pe.wait_ge(o_low[l], NQ // 2 * (GROUPS[c][-1] + 1))
                    for dc in range(KD):
                        if c + 1 < NC:
                            pe.wait_ge(qk_act[l], 2 * KO * (c + 2) - 3 + dc)
                        else:
                            pe.wait_ge((v_act, v_dve)[dc][l], NG)
                        split_products(pe, BD[dc][:, 0:w],
                                       lambda i: [weight(o_w, k, D)[:, i, dc * P:(dc + 1) * P] for k in range(2)],
                                       lambda i: hidden(c % 2, i, 0, w), KO, out_mm[l])

                project_qk(0, range(2 * KO))
                project_v(0)
                for c in range(NC):
                    mine, steps = quads(c)
                    for q, k, ms in steps:
                        project_qk(c + 1, ms)
                        if q in mine:
                            scores(q)
                            if q % NQ == 0 and q > 0:
                                project_v(q // NQ)
                        if q - LAG in mine:
                            transposes(q - LAG)
                        if q - LAG - VLAG in mine:
                            values(q - LAG - VLAG)
                    if c == NC - 1:
                        pe.wait_ge(t_dve[l], len(QUADS))
                        mean(2 * l + 1, NC - 2)
                    project_out(c)

            pe.wait_ge(*piece_split(0))
            embed(0)
            embed(1)
            pe.wait_ge(consts, 1)
            mean(0, 0)
            embed(2)
            variance(0, 0)
            mean(0, 1)
            embed(3)
            variance(0, 1)
            attention(0, 0)

            def ff_up(c):
                a, w = CHUNKS[c]
                pe.wait_ge(ln_out[1], c + 1)
                if c == 0:
                    wait_weight(pe, W_FF)
                for m in range(KH):
                    s = KH * c + m
                    if s >= 4:
                        pe.wait_ge(ff_t, s - 3)
                    elif s < 2:
                        pe.wait_ge(h_attn[0], KD * (NC - 1) + s + 1)
                    if s == 0:
                        pe.wait_ge(b1_ready, 3)
                    pe.matmul(BH[s % 4][:, 0:w], b1r[:, m * P:(m + 1) * P], ones_r[:, 0:w], start=True, stop=False)
                    split_products(pe, BH[s % 4][:, 0:w],
                                   lambda i: [weight(W_FF, k, FF)[:, i, m * P:(m + 1) * P] for k in range(2)],
                                   lambda i: normed(i, slice(a, a + w)), KD, ff1_mm, first=False)
                    if c == 0 and m == 1:
                        variance(1, 2)
                        mean(1, 3)
                    if c == 0 and m == 3:
                        variance(1, 3)
                    if c >= 2 and m == 1:
                        ff_down(c - 2)
                    if c == 2 and m == KH - 1:
                        mean(2, 0)
                    if c == NC - 1 and m == KH - 2:
                        variance(2, 0)

            def ff_down(c):
                a, w = CHUNKS[c]
                pe.wait_ge(ff_hid, KH * (c + 1))
                if c == 0:
                    wait_weight(pe, W_FF + 1)
                for dc in range(KD):
                    if c >= 1:
                        pe.wait_ge(ff2_ev, KD * (c - 1) + dc + 1)
                    split_products(pe, BO[dc][:, 0:w],
                                   lambda i: [weight(W_FF + 1, k, D)[:, i, dc * P:(dc + 1) * P] for k in range(2)],
                                   lambda i: hidden(c % 2, i, 0, w), KH, ff2_mm)

            for c in range(NC):
                ff_up(c)
            ff_down(NC - 2)
            ff_down(NC - 1)
            attention(1, 2)

            def router():
                pe.wait_ge(params, 5)
                for g in range(NG):
                    pe.wait_ge(ln_out[3], g // GC + 1)
                    split_products(pe, BO[0][0:NTOK[g], g * E:(g + 1) * E],
                                   lambda i: normed(i, cols(g)),
                                   lambda i: [gateR[:, k, i * E:(i + 1) * E] for k in range(2)], KD,
                                   log_mm)

            def sum_counts(i):
                pe.wait_ge(cnt_ready, i + 1)
                pe.matmul(BT[1][:, 0:1], mean_w[:, :], count[:, i % 2:i % 2 + 1], start=True,
                          stop=True).then_inc(cnt_mm, 1)

            def moe_up(e, c):
                a, w = MCHUNKS[c]
                if c == 0:
                    wait_weight(pe, W_MOE + 2 * e)
                if e == 0:
                    pe.wait_ge(ln_out[3], c + 1)
                for m in range(KH):
                    s = (e * NC + c) * KH + m
                    if s >= 4:
                        pe.wait_ge(m_gelu, s - 3)
                    elif s < 2:
                        pe.wait_ge(h_attn[1], KD * (NC - 1) + s + 1)
                    split_products(pe, BH[s % 4][:, 0:w],
                                   lambda i: [weight(W_MOE + 2 * e, k, FF)[:, i, m * P:(m + 1) * P] for k in range(2)],
                                   lambda i: normed(i, slice(a, a + w)), KD, m1_mm)
                    if s == 1:
                        variance(3, 2)
                        mean(3, 3)
                    if s == 4:
                        variance(3, 3)
                    n = e * NC + c
                    if m % 2 and 1 <= n <= 5:
                        i = 8 * (n - 1) + m // 2 - 1
                        if 0 <= i < 32:
                            sum_counts(i)

            def spread_gates(e):
                for c, (a, w) in enumerate(MCHUNKS):
                    j = e * NC + c
                    if j >= 2:
                        pe.wait_ge(gb_act, j - 1)
                    for g in range(a // GW, (a + w - 1) // GW + 1):
                        lo, hi = max(a, g * GW), min(a + w, (g + 1) * GW)
                        nt = NTOK[g]
                        mm = pe.matmul(BT[j % 2][:, lo - a:hi - a],
                                       gates[0:nt, g * E + e:g * E + e + 1].to_broadcast([nt, P]),
                                       ident[0:nt, lo - g * GW:hi - g * GW], start=True, stop=True)
                    mm.then_inc(gb_mm, 1)

            def moe_down(e, c):
                a, w = MCHUNKS[c]
                j = e * NC + c
                pe.wait_ge(m_hid, KH * (j + 1))
                if c == 0:
                    wait_weight(pe, W_MOE + 2 * e + 1)
                for dc in range(KD):
                    if j >= 1:
                        pe.wait_ge(m_y, KD * (j - 1) + dc + 1)
                    split_products(pe, BO[dc][:, 0:w],
                                   lambda i: [weight(W_MOE + 2 * e + 1, k, D)[:, i, dc * P:(dc + 1) * P]
                                              for k in range(2)],
                                   lambda i: hidden(j % 2, i, 0, w), KH, m2_mm,
                                   between=(lambda: sum_counts(8 * j + 3 + 2 * dc)) if e == 0 else None)
                    if e == 0:
                        sum_counts(8 * j + 4 + 2 * dc)

            steps = [(e, c) for e in range(E) for c in range(NC)]
            for n, (e, c) in enumerate(steps):
                moe_up(e, c)
                if n == 0:
                    router()
                if n == NC + 1:
                    pe.wait_ge(gates_ready, 1)
                    spread_gates(0)
                if c == 1 and e >= 1:
                    spread_gates(e)
                if n >= 1:
                    moe_down(*steps[n - 1])
            moe_down(*steps[-1])

        @block.scalar
        def _(act):
            def high_part(i):
                landed(act, i)
                if place_free(i):
                    act.wait_ge(*place_free(i))
                nc.scalar.activation(piece_place(i)[0], piece_raw(i), ACT.Copy).then_inc(high_ready, 1)

            for i in range(FIRST_W):
                high_part(i)
            act.wait_ge(consts, 8)
            act.wait_ge(small_in, 16)

            def square(n, c):
                w = CHUNKS[c][1]
                act.wait_ge(ln_xc[n], c + 1)
                if c >= 1:
                    act.wait_ge(ln_var[n], c)
                nc.scalar.activation(sq[:, :, 0:w], xc[:, :, 0:w], ACT.Square).then_inc(ln_sq[n], 1)

            def inv_root(n, c):
                w = CHUNKS[c][1]
                act.wait_ge(ln_var[n], c + 1)
                if c >= 1:
                    act.wait_ge(ln_out[n], c)
                nc.scalar.activation(rt[:, 0:w], BT[1][:, 0:w], ACT.Ln,
                                     bias=c_eps[:, 0:1]).then_inc(ln_ln[n], 1)
                act.wait_ge(ln_ln[n], c + 1)
                nc.scalar.activation(rs[:, 0:w], rt[:, 0:w], ACT.Exp, scale=-0.5).then_inc(ln_rs[n], 1)

            def attention(l):
                def move_q(c, ms):
                    if not ms:
                        return
                    w = CHUNKS[c][1]
                    means, variances = qk_sides(l, c)
                    for m in ms:
                        act.wait_ge(qk_mm[l], 2 * KO * c + m + 1)
                        nc.scalar.activation(work[:, m, 0:w], BH[m % 4][:, 0:w], ACT.Copy).then_inc(qk_act[l], 1)
                        if l == 0 and c == 0 and m == 7:
                            high_part(FIRST_W + 3)
                        if m - 1 in means:
                            square(*means[m - 1])
                        if c == 0 and m in variances:
                            inv_root(*variances[m])

                def move_v(g):
                    act.wait_ge(v_mm[l], 2 * g + 1)
                    if g >= 2:
                        act.wait_ge(o_mm[l], NQ * (g - 1))
                    nc.scalar.activation(vbuf[0:NTOK[g], g % 2, 0:512], BD[0][0:NTOK[g], :],
                                         ACT.Copy).then_inc(v_act[l], 1)

                def exps(q):
                    c, g, t = QUADS[q]
                    nt = NTOK[g]
                    act.wait_ge(s_max[l], q + 1)
                    if q >= 4:
                        act.wait_ge(t_mm[l], q - 3)
                    for i in range(QH):
                        k = QH * (q % 4) + i
                        nc.scalar.activation(probs[0:nt, q % 4, i * GW:i * GW + nt],
                                             BS[q % 2][0:nt, i * GW:i * GW + nt], ACT.Exp,
                                             bias=negmax[0:nt, k:k + 1], scale=DH ** -0.5,
                                             accum_out=sums[0:nt, k:k + 1]).then_inc(s_exp[l], 1)

                def high_out(pair):
                    c, g, t = QUADS[2 * pair]
                    nt, a = NTOK[g], g * GW - CHUNKS[c][0]
                    act.wait_ge(o_mm[l], 2 * pair + 2)
                    if c >= 2:
                        act.wait_ge(out_mm[l], KD * (c - 1))
                    nc.scalar.activation(heads_out(0, c, t, a, nt), out_pair(pair, nt),
                                         ACT.Copy).then_inc(o_high[l], 1)

                move_q(0, range(2 * KO))
                move_v(0)
                for c in range(NC):
                    mine, steps = quads(c)
                    if c == NC - 1:
                        high_part(FIRST_W + W_QKVO[l] + 4)
                        high_part(FIRST_W + W_QKVO[l] + 5)
                    for q, k, ms in steps:
                        move_q(c + 1, ms)
                        if q in mine:
                            exps(q)
                            if q % NQ == 0 and q > 0:
                                move_v(q // NQ)
                        if q - LAG - VLAG in mine and (q - LAG - VLAG) % 2:
                            high_out((q - LAG - VLAG) // 2)
                    if c + 1 < NC:
                        for side in qk_sides(l, c + 1)[1].values():
                            inv_root(*side)
                square(2 * l + 1, NC - 2)

            square(0, 0)
            high_part(FIRST_W)
            inv_root(0, 0)
            high_part(FIRST_W + 1)
            square(0, 1)
            inv_root(0, 1)
            high_part(FIRST_W + 2)
            attention(0)

            def ff_load(s):
                v = ff_bufs(s // 2)[0][:, s % 2, :]
                act.wait_ge(ff1_mm, s + 1)
                if s // 2 >= 3:
                    act.wait_ge(ff_z, s // 2 - 2)
                nc.scalar.activation(v, BH[s % 4][:, 0:CHUNKS[s // KH][1]], ACT.Identity,
                                     bias=c_magic[:, 0:1], scale=UNIT).then_inc(ff_t, 1)

            def ff_distance(p):
                v, a, y1, y0 = ff_bufs(p)
                act.wait_ge(ff_t, 2 * p + 2)
                if p >= 3:
                    act.wait_ge(ff_q, p - 2)
                nc.scalar.activation(a, v, ACT.Abs, bias=c_magic[:, 1:2]).then_inc(ff_abs, 1)

            def ff_knots(p):
                v, a, y1, y0 = ff_bufs(p)
                act.wait_ge(ff_knot, p + 1)
                if p >= 3:
                    act.wait_ge(ff_hid, 2 * (p - 2))
                nc.scalar.activation(y0, y1, ACT.Gelu, bias=c_knot0[:, 0:1], scale=-1.0 / UNIT).then_inc(ff_y0, 1)
                act.wait_ge(ff_frac, p + 1)
                act.wait_ge(ff_y0, p + 1)
                nc.scalar.activation(y1, y1, ACT.Gelu, bias=c_knot1[:, 0:1], scale=-1.0 / UNIT).then_inc(ff_y1, 1)

            def ff_high(p):
                c = 2 * p // KH
                act.wait_ge(ff_z, p + 1)
                if c >= 2:
                    act.wait_ge(ff2_mm, KD * (c - 1))
                nc.scalar.activation(ff_rows(p, 0), ff_bufs(p)[3], ACT.Identity,
                                     bias=c_magic[:, 1:2]).then_inc(ff_hi, 1)

            for p in range(-1, NP + 2):
                if p >= 2:
                    ff_high(p - 2)
                if 0 <= p < NP:
                    ff_knots(p)
                if p + 1 < NP:
                    ff_load(2 * p + 2)
                    ff_load(2 * p + 3)
                    ff_distance(p + 1)
                if p == -1:
                    inv_root(1, 2)
                    square(1, 3)
                    inv_root(1, 3)
                if p in (KH // 2, KH):
                    high_part(FIRST_W + W_FF + 1 + 2 * p // KH)
                if p == 3 * KH // 2:
                    square(2, 0)
            inv_root(2, 0)
            for i in (8, 9):
                high_part(FIRST_W + i)
            attention(1)
            inv_root(3, 2)
            square(3, 3)

            def spread(e):
                for c, (a, w) in enumerate(MCHUNKS):
                    j = e * NC + c
                    act.wait_ge(gb_mm, j + 1)
                    if e >= 2:
                        act.wait_ge(m_y, KD * ((e - 2) * NC + c + 1))
                    nc.scalar.activation(moe_gate(e, c)[:, 0:w], BT[j % 2][:, 0:w], ACT.Copy).then_inc(gb_act, 1)

            for s in range(E * NC * KH):
                e, c, m = s // (NC * KH), s // KH % NC, s % KH
                w = MCHUNKS[c][1]
                act.wait_ge(m1_mm, s + 1)
                if s == 6:
                    inv_root(3, 3)
                if s in (10, 12):
                    high_part(FIRST_W + W_MOE + s // 2 - 3)
                if e >= 1 and e + 1 < E and (c, m) in ((0, 1), (1, 4)):
                    high_part(FIRST_W + W_MOE + 2 * e + 2 + c)
                if s >= 4:
                    act.wait_ge(m_hid, s - 3)
                nc.scalar.activation(moe_g(s)[:, 0:w], BH[s % 4][:, 0:w], ACT.Gelu_apprx_tanh,
                                     bias=prm[:, S_B1M + e * KH + m:S_B1M + e * KH + m + 1]).then_inc(m_gelu, 1)
                if c == 1 and m == KH - 1 and e >= 1:
                    if e == 1:
                        spread(0)
                    spread(e)

        @block.vector
        def _(dve):
            done = [0]

            def tick(ins):
                done[0] += 1
                ins.then_inc(dve_line, 1)
                return done[0]

            def link(ins):
                dve.wait_ge(dve_line, tick(ins))

            dve.wait_ge(small_in, 16)
            pos = prm[:, S_POS:S_CLS].rearrange("p (k n) -> p k n", k=KD)
            for k in range(KD):
                nc.vector.tensor_scalar(addT[:, k, 1:TOK], pos[:, k, 1:TOK], prm[:, S_BLIN + k:S_BLIN + k + 1],
                                        None, ALU.add).then_inc(params, 1)
            nc.vector.tensor_tensor(addT[:, :, 0], pos[:, :, 0], prm[:, S_CLS:S_BLIN], ALU.add).then_inc(params, 1)
            tick(nc.vector.tensor_scalar(b2u[:, :], prm[:, S_B2F:S_B1M], UNIT, None, ALU.mult))
            nc.vector.tensor_copy(gateR[:, 0, :], prm[:, S_GATE:S_END]).then_inc(params, 1)
            dve.wait_ge(params, 4)
            nc.vector.tensor_tensor(gateR[:, 1, :], prm[:, S_GATE:S_END], gateR[:, 0, :].bitcast(F32),
                                    ALU.subtract).then_inc(params, 1)
            nc.vector.memset(h[:, :, 0:(NG - 1) * GW].rearrange("p k (g n) -> p k g n", n=GW)[:, :, :, GW - 1:GW],
                             0.0)

            def low_part(i):
                dve.wait_ge(high_ready, i + 1)
                high, low = piece_place(i)
                nc.vector.tensor_tensor(low, piece_raw(i), high.bitcast(F32), ALU.subtract).then_inc(start_split, 1)

            def set_h(c):
                for dc in range(KD):
                    dve.wait_ge(emb_mm, KD * c + dc + 1)
                    for g in GROUPS[c]:
                        ni = NTOK[g] // TOK
                        a = g * GW - CHUNKS[c][0]
                        ins = nc.vector.tensor_tensor(
                            h[:, dc, cols(g)].rearrange("p (i n) -> p i n", n=TOK),
                            BD[dc][:, a:a + NTOK[g]].rearrange("p (i n) -> p i n", n=TOK),
                            addT[:, dc:dc + 1, :].to_broadcast([P, ni, TOK]), ALU.add)
                    ins.then_inc(h_set, 1)

            def center(n, c):
                a, w = CHUNKS[c]
                dve.wait_ge(ln_mean[n], c + 1)
                if c >= 1:
                    dve.wait_ge(ln_out[n], c)
                elif n >= 1:
                    dve.wait_ge(ln_out[n - 1], NC)
                mean = BT[0][:, 0:w].rearrange("p (a n) -> p a n", a=1).to_broadcast([P, KD, w])
                nc.vector.tensor_tensor(xc[:, :, 0:w], h[:, :, a:a + w], mean,
                                        ALU.subtract).then_inc(ln_xc[n], 1)

            def finish(n, c):
                a, w = CHUNKS[c]
                dve.wait_ge(ln_rs[n], c + 1)
                r, t = rs[:, 0:w], rt[:, 0:w]
                link(nc.vector.tensor_tensor(t, r, r, ALU.mult))
                link(nc.vector.scalar_tensor_tensor(t, BT[1][:, 0:w], EPS, t, ALU.add, ALU.mult))
                link(nc.vector.tensor_scalar(t, t, -0.5, 1.5, ALU.mult, ALU.add))
                link(nc.vector.tensor_tensor(r, t, r, ALU.mult))
                x2 = xc[:, :, 0:w]
                rb = rs[:, 0:w].rearrange("p (a n) -> p a n", a=1).to_broadcast([P, KD, w])
                link(nc.vector.tensor_tensor(x2, x2, rb, ALU.mult))
                link(nc.vector.tensor_copy(xn[:, 0, :, a:a + w], x2))
                nc.vector.tensor_tensor(xn[:, 1, :, a:a + w], x2, xn[:, 0, :, a:a + w].bitcast(F32),
                                        ALU.subtract).then_inc(ln_out[n], 1)

            low_part(0)
            low_part(1)
            dve.wait_ge(params, 3)
            for c in range(NC):
                low_part(c + 2)
                set_h(c)
                if c >= 2:
                    finish(0, c - 2)
                if c >= 1 and c <= 2:
                    center(0, c - 1)
            def prepare():
                dve.wait_ge(mats_in, 64)
                nc.vector.tensor_copy(identb[:, :], ident[:, :]).then_inc(masks, 1)
                for l in range(2):
                    for i in range(QH):
                        ins = nc.vector.tensor_copy(maskb[:, l, i, :], maskf[:, l, :])
                ins.then_inc(masks, 1)
                dve.wait_ge(emb_mm, KD * NC)
                nc.vector.memset(
                    hid[:, :, :, :].rearrange("p s k (m n) -> p (s k m) n", n=GW)[:, :, GW - 1:GW].bitcast(F32), 0.0)
                dve.wait_ge(consts, 8)
                for row in (0, BL):
                    nc.vector.tensor_copy(b1r[row:row + 1, :], b1row[row:row + 1, :]).then_inc(b1_ready, 1)
                dve.wait_ge(b1_ready, 2)
                low = b1r[BL:BL + 1, :]
                nc.vector.tensor_tensor(low, b1row[BL:BL + 1, :], low.bitcast(F32), ALU.subtract).then_inc(b1_ready, 1)

            def attention(l):
                def move_v(g):
                    dve.wait_ge(v_mm[l], 2 * g + 2)
                    if g >= 2:
                        dve.wait_ge(o_mm[l], NQ * (g - 1))
                    nc.vector.tensor_copy(vbuf[0:NTOK[g], g % 2, 512:HD], BD[1][0:NTOK[g], :]).then_inc(v_dve[l], 1)

                def row_max(q):
                    c, g, t = QUADS[q]
                    nt = NTOK[g]
                    dve.wait_ge(s_mm[l], q + 1)
                    k = QH * (q % 4)
                    link(nc.vector.tensor_reduce(
                        maxes[0:nt, k:k + QH],
                        BS[q % 2][0:nt, 0:QH * GW].rearrange("p (h n) -> p h n", h=QH)[:, :, 0:nt], AX_X, ALU.max))
                    nc.vector.tensor_scalar(negmax[0:nt, k:k + QH], maxes[0:nt, k:k + QH], -DH ** -0.5, None,
                                            ALU.mult).then_inc(s_max[l], 1)

                def invert_sums(q):
                    c, g, t = QUADS[q]
                    nt, k = NTOK[g], QH * (q % 4)
                    dve.wait_ge(s_exp[l], QH * (q + 1))
                    nc.vector.reciprocal(rsum[0:nt, k:k + QH], sums[0:nt, k:k + QH]).then_inc(s_inv[l], 1)

                def move_t(q):
                    c, g, t = QUADS[q]
                    nt = NTOK[g]
                    dve.wait_ge(t_mm[l], q + 1)
                    if q >= 2:
                        dve.wait_ge(o_mm[l], q - 1)
                    nc.vector.tensor_copy(
                        probsT[0:nt, q % 2, :].rearrange("p (h n) -> p h n", h=QH)[:, :, 0:nt],
                        BT[q % 2][0:nt, 0:QH * GW].rearrange("p (h n) -> p h n", h=QH)[:, :, 0:nt],
                    ).then_inc(t_dve[l], 1)

                def low_out(pair):
                    c, g, t = QUADS[2 * pair]
                    nt, a = NTOK[g], g * GW - CHUNKS[c][0]
                    dve.wait_ge(o_high[l], pair + 1)
                    nc.vector.tensor_tensor(heads_out(1, c, t, a, nt), out_pair(pair, nt),
                                            heads_out(0, c, t, a, nt).bitcast(F32),
                                            ALU.subtract).then_inc(o_low[l], 1)

                def add_out(c):
                    a, w = CHUNKS[c]
                    for dc in range(KD):
                        dve.wait_ge(out_mm[l], KD * c + dc + 1)
                        if l == 0:
                            ins = nc.vector.tensor_tensor(h[:, dc, a:a + w], BD[dc][:, 0:w], h[:, dc, a:a + w],
                                                          ALU.add)
                        else:
                            ins = nc.vector.scalar_tensor_tensor(
                                h[:, dc, a:a + w], BD[dc][:, 0:w], prm[:, S_BO + dc:S_BO + dc + 1],
                                h[:, dc, a:a + w], ALU.add, ALU.add)
                        ins.then_inc(h_attn[l], 1)

                for side in qk_sides(l, 0)[0].values():
                    center(*side)
                    finish(*side)
                if l == 0:
                    prepare()
                move_v(0)
                for c in range(NC):
                    mine, steps = quads(c)
                    sides = list(qk_sides(l, c + 1)[0].values()) if c + 1 < NC else []
                    for q, k, ms in steps:
                        if q in mine:
                            row_max(q)
                        if q - LAG in mine:
                            move_t(q - LAG)
                        if q - 1 in mine:
                            invert_sums(q - 1)
                        if q in mine and q % NQ == 0 and q > 0:
                            move_v(q // NQ)
                        if sides and k == LAG + VLAG - 1:
                            center(*sides[0])
                        if q - LAG - VLAG in mine and (q - LAG - VLAG) % 2:
                            low_out((q - LAG - VLAG) // 2)
                    for side in sides:
                        finish(*side)
                    if c == NC - 1:
                        center(2 * l + 1, NC - 2)
                    add_out(c)

            attention(0)

            def ff_find(p):
                v, a, kn, y0 = ff_bufs(p)
                dve.wait_ge(ff_abs, p + 1)
                if p >= 3:
                    dve.wait_ge(ff_lin, p - 2)
                nc.vector.tensor_scalar(kn, a, -(KNOT - 1) / 2, MAGIC_KNOT, ALU.add, ALU.add).then_inc(ff_knot, 1)
                dve.wait_ge(ff_knot, p + 1)
                nc.vector.scalar_tensor_tensor(a, kn, MAGIC_KNOT, a, ALU.subtract, ALU.subtract).then_inc(ff_frac, 1)
                nc.vector.tensor_scalar(v, v, MAGIC, None, ALU.max).then_inc(ff_pos, 1)

            def ff_interp(p):
                v, a, dy, y0 = ff_bufs(p)
                dve.wait_ge(ff_lin, p + 1)
                nc.vector.scalar_tensor_tensor(y0, y0, KNOT, a, ALU.mult, ALU.subtract).then_inc(ff_q, 1)

            def ff_round(p):
                v, a, dy, y0 = ff_bufs(p)
                dve.wait_ge(ff_q, p + 1)
                dve.wait_ge(ff_pos, p + 1)
                nc.vector.scalar_tensor_tensor(y0, y0, UNIT / KNOT, v, ALU.mult, ALU.add).then_inc(ff_z, 1)

            def ff_low(p):
                dve.wait_ge(ff_hi, p + 1)
                nc.vector.scalar_tensor_tensor(ff_rows(p, 1), ff_bufs(p)[3], MAGIC, ff_rows(p, 0).bitcast(F32),
                                               ALU.subtract, ALU.subtract).then_inc(ff_hid, 2)

            def ff_out(c):
                a, w = CHUNKS[c]
                for dc in range(KD):
                    dve.wait_ge(ff2_mm, KD * c + dc + 1)
                    t = rt[:, 0:w]
                    nc.vector.tensor_scalar(t, BO[dc][:, 0:w], b2u[:, dc:dc + 1], MAGIC, ALU.add,
                                            ALU.add).then_inc(ff2_ev, 1)
                    dve.wait_ge(ff2_ev, KD * c + dc + 1)
                    link(nc.vector.tensor_scalar(t, t, MAGIC, 1.0 / UNIT, ALU.subtract, ALU.mult))
                    nc.vector.tensor_tensor(h[:, dc, a:a + w], h[:, dc, a:a + w], t, ALU.add).then_inc(h_ff, 1)
                    dve.wait_ge(h_ff, KD * c + dc + 1)

            for p in range(NP + 2):
                if p < NP:
                    ff_find(p)
                if p >= 2:
                    ff_low(p - 2)
                if 1 <= p <= NP:
                    ff_interp(p - 1)
                if 1 <= p <= NP:
                    ff_round(p - 1)
                if p == 0:
                    finish(1, 2)
                    center(1, 3)
                    finish(1, 3)
                if KH <= p < NP and p % (KH // 2) == 0:
                    ff_out(2 * p // KH - 2)
                if p == 3 * KH // 2:
                    center(2, 0)
            finish(2, 0)
            ff_out(NC - 2)
            ff_out(NC - 1)
            attention(1)
            finish(3, 2)
            center(3, 3)
            dve.wait_ge(o_mm[1], len(QUADS))
            for t, value in ((logits, BIG), (keys, BIG), (gates, 0.0)):
                last = tick(nc.vector.memset(t, value))
            dve.wait_ge(dve_line, last)

            full = (NG - 1) * E

            def start_search():
                dve.wait_ge(log_mm, NG)
                link(nc.vector.tensor_copy(logits[0:NTOK[0], 0:full], BO[0][0:NTOK[0], 0:full]))
                link(nc.vector.tensor_copy(logits[0:NTOK[-1], full:], BO[0][0:NTOK[-1], full:NG * E]))
                link(nc.vector.memset(found[:, :], 0))

            def search(i):
                if i > 0:
                    judge(i - 1)
                if i == 32:
                    return
                if i > 0:
                    bit = 31 - i
                    link(nc.vector.tensor_scalar(tryb[:, :], found[:, :], 1 << bit, None, ALU.bitwise_or))
                src, than = (logits, 0.0) if i == 0 else (keys, tryb[:, 0:1].bitcast(F32))
                nc.vector.tensor_scalar(below, src[:, :], than, None, ALU.is_lt, ALU.add,
                                        accum_out=count[:, i % 2:i % 2 + 1]).then_inc(cnt_ready, 1)

            def judge(i):
                bit = 31 - i
                dve.wait_ge(cnt_mm, i + 1)
                total = BT[1][:, 0:1]
                if i == 0:
                    link(nc.vector.tensor_scalar(sign[:, :], total, TOPK / D, -2.0, ALU.is_ge, ALU.mult))
                    link(nc.vector.tensor_scalar(sign[:, :], sign[:, :], 1.0, None, ALU.add))
                    link(nc.vector.tensor_scalar(rank[:, :], sign[:, :], (2 * TOPK - NLOG - 1) / (2 * D),
                                                 (NLOG + 1) / (2 * D), ALU.mult, ALU.add))
                    for rows, a, b in ((NTOK[0], 0, full), (NTOK[-1], full, NG * E)):
                        link(nc.vector.tensor_scalar(keys[0:rows, a:b], logits[0:rows, a:b], sign[0:rows, 0:1],
                                                     None, ALU.mult))
                else:
                    link(nc.vector.tensor_scalar(newb[:, :], total, rank[:, 0:1], float(1 << bit), ALU.is_lt,
                                                 ALU.mult))
                    link(nc.vector.tensor_tensor(found[:, :], found[:, :], newb[:, :], ALU.bitwise_or))

            def gate():
                link(nc.vector.tensor_scalar(kth[:, :], found[:, :].bitcast(F32), sign[:, 0:1], None, ALU.mult))
                link(nc.vector.scalar_tensor_tensor(gates[0:NTOK[0], 0:full], logits[0:NTOK[0], 0:full],
                                                    kth[0:NTOK[0], 0:1], logits[0:NTOK[0], 0:full],
                                                    ALU.is_ge, ALU.mult))
                nc.vector.scalar_tensor_tensor(gates[0:NTOK[-1], full:], logits[0:NTOK[-1], full:],
                                               kth[0:NTOK[-1], 0:1], logits[0:NTOK[-1], full:],
                                               ALU.is_ge, ALU.mult).then_inc(gates_ready, 1)

            def moe_split(s):
                c, m = s // KH % NC, s % KH
                w = MCHUNKS[c][1]
                j = s // KH
                dve.wait_ge(m_gelu, s + 1)
                if j >= 2:
                    dve.wait_ge(m2_mm, KD * (j - 1))
                high, low = (hid[:, j % 2, k, m * CW:m * CW + w] for k in range(2))
                nc.vector.tensor_copy(high, moe_g(s)[:, 0:w]).then_inc(m_high, 1)
                dve.wait_ge(m_high, s + 1)
                nc.vector.tensor_tensor(low, moe_g(s)[:, 0:w], high.bitcast(F32), ALU.subtract).then_inc(m_hid, 1)

            def moe_out(e, c):
                for dc in range(KD):
                    moe_out1(e, c, dc)

            def moe_out1(e, c, dc):
                w = MCHUNKS[c][1]
                j = (e * NC + c) * KD + dc
                dve.wait_ge(m2_mm, j + 1)
                if e == 0:
                    nc.vector.tensor_scalar(moe_y0(j)[:, 0:w], BO[dc][:, 0:w],
                                            prm[:, S_B2M + dc * E:S_B2M + dc * E + 1], None,
                                            ALU.add).then_inc(m_y, 1)
                    return
                dve.wait_ge(gb_act, e * NC + c + 1)
                dve.wait_ge(h_moe, max(j - 3, 1))
                nc.vector.scalar_tensor_tensor(
                    moe_y(j)[:, 0:w], BO[dc][:, 0:w], prm[:, S_B2M + dc * E + e:S_B2M + dc * E + e + 1],
                    moe_gate(e, c)[:, 0:w], ALU.add, ALU.mult).then_inc(m_y, 1)

            steps = [(e, c) for e in range(E) for c in range(NC)]
            for s in range(E * NC * KH):
                n, m = s // KH, s % KH
                moe_split(s)
                if s == 5:
                    finish(3, 3)
                if s == KH - 1:
                    start_search()
                if m % 2 == 0 and 1 <= n <= 4:
                    search(8 * (n - 1) + m // 2)
                if m == KH - 1 and 1 <= n <= 4:
                    for i in range(4, 8):
                        search(8 * (n - 1) + i)
                        if i % 2:
                            moe_out1(*steps[n - 1], (i - 4) // 2)
                if n == 5 and m == 1:
                    search(32)
                    gate()
                if s % KH == 4 and s >= (NC + 2) * KH:
                    moe_out(*steps[s // KH - 2])
            moe_out(*steps[-2])
            moe_out(*steps[-1])


def layout(i):
    import numpy as np

    def rows(a):
        k = a.shape[0] // P
        return a.reshape(k, P, -1).transpose(1, 0, 2).reshape(P, -1)

    i = {k: np.asarray(v) for k, v in i.items()}
    col = np.array([g * GW + t for g in range(NG) for t in range(NTOK[g])])
    patch = np.array([c for n, c in enumerate(col) if n % TOK])
    px = i["x"].reshape(B, C, SIDE, PATCH, SIDE, PATCH).transpose(1, 3, 5, 0, 2, 4).reshape(C * PATCH * PATCH, -1)
    xt = np.zeros((C * PATCH * PATCH, T), np.float32)
    xt[:, patch] = px
    a = {"x": xt.reshape(KF, P, T).transpose(1, 0, 2), "w_lin": rows(i["L0_tok_W_lin"].T)}
    a["attn0"] = np.stack([rows(i[f"L0_attn_w{n}"].reshape(HD, D).T) for n in "qkv"]
                          + [rows(i["L0_attn_wo"].T)])
    a["ffn"] = np.stack([rows(i["L0_ffn_w1"]), rows(i["L0_ffn_w2"])])
    a["attn1"] = np.stack([rows(i[f"L1_attn_W{n}"]) for n in "qkvo"])
    w1, w2 = i["L1_ffn_w1"], i["L1_ffn_w2"]
    a["moe"] = np.stack([rows(w.T) for e in range(E) for w in (w1[e], w2[e])])
    a["small"] = np.concatenate(
        [rows(i["L0_tok_position_embeddings"][0].T)]
        + [rows(v.reshape(-1, 1)) for v in (i["L0_tok_class_token"], i["L0_tok_b_lin"], i["L1_attn_bo"],
                                            i["L0_ffn_b1"], i["L0_ffn_b2"])]
        + [rows(i["L1_ffn_b1"][e].reshape(-1, 1)) for e in range(E)]
        + [rows(i["L1_ffn_b2"].T), rows(i["L1_ffn_gate_weight"].T)], axis=1)
    t = np.arange(P)
    same = (t[:, None] // TOK == t[None, :] // TOK)[:, :GW]
    late = (t[None, :] > t[:, None])[:, :GW]
    a["b1"] = i["L0_ffn_b1"].reshape(1, FF)
    a["ident"] = np.eye(P, dtype=np.float32)
    a["mask"] = np.stack([np.where(same & ~late, 0.0, -1e30), np.where(same, 0.0, -1e30)],
                         axis=1).astype(np.float32)
    return {f"in_{k}": np.ascontiguousarray(v) for k, v in a.items()}, col


def kernel(**inputs):
    import concourse.bacc as bacc
    from concourse.bass_utils import run_bass_kernel_spmd

    arrays, col = layout(inputs)
    nc = bacc.Bacc("TRN2", target_bir_lowering=False, num_devices=1)
    args = {n: nc.dram_tensor(n, a.shape, F32, kind="ExternalInput").ap() for n, a in arrays.items()}
    out = nc.dram_tensor("out", (P, KD, T), F32, kind="ExternalOutput").ap()
    weights = [args[f"in_{name}"][i] for name in ("attn0", "ffn", "attn1", "moe")
               for i in range(arrays[f"in_{name}"].shape[0])]
    vit_tower(nc, args["in_x"], args["in_w_lin"], weights, args["in_small"], args["in_ident"],
              args["in_mask"], args["in_b1"], out)
    r = run_bass_kernel_spmd(nc, [arrays], core_ids=[0])
    got = r.results[0]["out"]
    return got.transpose(2, 1, 0).reshape(T, D)[col].reshape(B, TOK, D)
```
